# Optimizing a Trainium2 kernel written in Bass

```python
import numpy as np
import jax
import jax.numpy as jnp

def _softmax(x, axis=-1):
    return jax.nn.softmax(x, axis=axis)

def _gelu(x):
    return jax.nn.gelu(x, approximate=True)

def _silu(x):
    return jax.nn.silu(x)

def _sigmoid(x):
    return jax.nn.sigmoid(x)

def _layernorm(x, axis=-1, eps=1e-05):
    m = jnp.mean(x, axis=axis, keepdims=True)
    v = jnp.var(x, axis=axis, keepdims=True)
    return (x - m) / jnp.sqrt(v + eps)

def _scatter_add(tgt, idx, src, axis=0):
    return tgt.at[idx].add(src)

def _segment_sum(src, seg, n):
    return jax.ops.segment_sum(src, seg, n)
kernel_name = 'mk_adj_preln_d4_adj_r2_3a73e0'

def setup_inputs(seed: int=0):
    np.random.seed(seed)
    _w = jnp.asarray

    def _rec_inputs():
        import jax
        import jax.numpy as jnp
        _gk = jax.random.key(seed)
        x = -0.0002928 + 1 * jax.random.normal(jax.random.fold_in(_gk, 1), (16, 512, 128), jnp.float32)
        _a = jax.random.bernoulli(jax.random.fold_in(_gk, 2), 0.0078125, (16, 512, 512))
        _a = jnp.logical_or(_a, jnp.swapaxes(_a, -1, -2))
        _a = jnp.logical_or(_a, jnp.eye(512, dtype=bool))
        adj = _a.astype(jnp.int32)
        return (x, adj)
    x, adj = _rec_inputs()

    def _L0_gnn_setup():
        import jax, jax.numpy as jnp
        import numpy as np
        B, N, F_IN, F_OUT = (8, 1024, 128, 128)
        ALPHA = 0.2
        key = jax.random.key(seed)
        k1, k2, k3, k4 = jax.random.split(key, 4)
        h = jax.random.normal(k1, (B, N, F_IN), dtype=jnp.float32)
        adj = jax.random.randint(k2, (B, N, N), 0, 2, dtype=jnp.int32)
        W = jax.random.normal(k3, (F_OUT, F_IN), dtype=jnp.float32) / np.sqrt(F_IN)
        a = jax.random.normal(k4, (1, 2 * F_OUT), dtype=jnp.float32) / np.sqrt(2 * F_OUT)
        return {'h': h, 'adj': adj, 'W': W, 'a': a}
    _L0_gnn_all = _L0_gnn_setup()
    _L0_gnn_in = {k: v for k, v in _L0_gnn_all.items() if k in ('W', 'a')}
    del _L0_gnn_all

    def _L1_gnn_setup():
        import jax, jax.numpy as jnp
        import numpy as np
        B, N, C_IN, H, C_OUT = (8, 512, 128, 4, 128)
        C = C_OUT // H
        ALPHA = 0.2
        NEG_INF = -9000000000000000.0
        key = jax.random.key(seed)
        k1, k2, k3, k4, k5 = jax.random.split(key, 5)
        node_feats = jax.random.normal(k1, (B, N, C_IN), dtype=jnp.float32)
        adj_matrix = jax.random.randint(k2, (B, N, N), 0, 2, dtype=jnp.int32)
        eye = jnp.eye(N, dtype=jnp.int32)[None]
        adj_matrix = jnp.maximum(adj_matrix, eye)

        def xavier(k, shape, fan_in, fan_out, gain=1.414):
            lim = gain * np.sqrt(6.0 / (fan_in + fan_out))
            return jax.random.uniform(k, shape, jnp.float32, -lim, lim)
        W = xavier(k3, (C_OUT, C_IN), C_IN, C_OUT)
        b = jnp.zeros((C_OUT,), dtype=jnp.float32)
        a = xavier(k4, (H, 2 * C), 2 * C, H)
        return {'node_feats': node_feats, 'adj_matrix': adj_matrix, 'W': W, 'b': b, 'a': a}
    _L1_gnn_all = _L1_gnn_setup()
    _L1_gnn_in = {k: v for k, v in _L1_gnn_all.items() if k in ('W', 'b', 'a')}
    del _L1_gnn_all

    def _L2_gnn_setup():
        import jax, jax.numpy as jnp
        import numpy as np
        B, S, D = (64, 256, 128)

        def _leaky(x):
            return jnp.where(x >= 0, x, 0.2 * x)
        key = jax.random.key(seed)
        k = jax.random.split(key, 6)
        stdv = 1.0 / np.sqrt(D)
        return {'hidden': jax.random.normal(k[0], (B, S, D), dtype=jnp.float32), 'adj': jax.random.randint(k[1], (B, S, S), 0, 5, dtype=jnp.int32), 'a0': jax.random.uniform(k[2], (D, 1), jnp.float32, -stdv, stdv), 'a1': jax.random.uniform(k[3], (D, 1), jnp.float32, -stdv, stdv), 'a2': jax.random.uniform(k[4], (D, 1), jnp.float32, -stdv, stdv), 'a3': jax.random.uniform(k[5], (D, 1), jnp.float32, -stdv, stdv), 'bias': jnp.zeros((D,), dtype=jnp.float32)}
    _L2_gnn_all = _L2_gnn_setup()
    _L2_gnn_in = {k: v for k, v in _L2_gnn_all.items() if k in ('a0', 'a1', 'a2', 'a3', 'bias')}
    del _L2_gnn_all

    def _L3_gnn_setup():
        import jax, jax.numpy as jnp
        import numpy as np
        OUT = 128
        NUM_LAYERS = 3

        def _gru_cell(inp, h, w_ih, w_hh, b_ih, b_hh):
            gi = inp @ w_ih.T + b_ih
            gh = h @ w_hh.T + b_hh
            i_r, i_z, i_n = jnp.split(gi, 3, axis=-1)
            h_r, h_z, h_n = jnp.split(gh, 3, axis=-1)
            r = jax.nn.sigmoid(i_r + h_r)
            z = jax.nn.sigmoid(i_z + h_z)
            n = jnp.tanh(i_n + r * h_n)
            return (1.0 - z) * n + z * h
        key = jax.random.key(seed)
        ks = jax.random.split(key, 8)
        B, N, D = (32, 256, 128)
        x = jax.random.normal(ks[0], (B, N, D), dtype=jnp.float32)
        adj = jax.random.randint(ks[1], (B, N, N), 0, 2, dtype=jnp.int32)
        s = 1.0 / np.sqrt(OUT)
        weight = jax.random.uniform(ks[2], (NUM_LAYERS, OUT, OUT), jnp.float32, -s, s)
        w_ih = jax.random.uniform(ks[3], (3 * OUT, OUT), jnp.float32, -s, s)
        w_hh = jax.random.uniform(ks[4], (3 * OUT, OUT), jnp.float32, -s, s)
        b_ih = jax.random.uniform(ks[5], (3 * OUT,), jnp.float32, -s, s)
        b_hh = jax.random.uniform(ks[6], (3 * OUT,), jnp.float32, -s, s)
        return {'x': x, 'adj': adj, 'weight': weight, 'w_ih': w_ih, 'w_hh': w_hh, 'b_ih': b_ih, 'b_hh': b_hh}
    _L3_gnn_all = _L3_gnn_setup()
    _L3_gnn_in = {k: v for k, v in _L3_gnn_all.items() if k in ('weight', 'w_ih', 'w_hh', 'b_ih', 'b_hh')}
    del _L3_gnn_all
    return {'x': x, 'adj': adj, 'L0_gnn_W': _L0_gnn_in['W'], 'L0_gnn_a': _L0_gnn_in['a'], 'L1_gnn_W': _L1_gnn_in['W'], 'L1_gnn_b': _L1_gnn_in['b'], 'L1_gnn_a': _L1_gnn_in['a'], 'L2_gnn_a0': _L2_gnn_in['a0'], 'L2_gnn_a1': _L2_gnn_in['a1'], 'L2_gnn_a2': _L2_gnn_in['a2'], 'L2_gnn_a3': _L2_gnn_in['a3'], 'L2_gnn_bias': _L2_gnn_in['bias'], 'L3_gnn_weight': _L3_gnn_in['weight'], 'L3_gnn_w_ih': _L3_gnn_in['w_ih'], 'L3_gnn_w_hh': _L3_gnn_in['w_hh'], 'L3_gnn_b_ih': _L3_gnn_in['b_ih'], 'L3_gnn_b_hh': _L3_gnn_in['b_hh']}

def reference(x, adj, L0_gnn_W, L0_gnn_a, L1_gnn_W, L1_gnn_b, L1_gnn_a, L2_gnn_a0, L2_gnn_a1, L2_gnn_a2, L2_gnn_a3, L2_gnn_bias, L3_gnn_weight, L3_gnn_w_ih, L3_gnn_w_hh, L3_gnn_b_ih, L3_gnn_b_hh):
    import jax
    import jax.numpy as jnp

    def _L0_gnn_ref(h, adj, W, a):
        import jax, jax.numpy as jnp
        import numpy as np
        B, N, F_IN, F_OUT = (8, 1024, 128, 128)
        ALPHA = 0.2
        Wh = jnp.einsum('bnf,of->bno', h, W)
        Fo = Wh.shape[-1]
        a1 = a[0, :Fo]
        a2 = a[0, Fo:]
        s1 = Wh @ a1
        s2 = Wh @ a2
        e = jax.nn.leaky_relu(s1[:, :, None] + s2[:, None, :], negative_slope=ALPHA)
        mask = adj == 0
        e = jnp.where(mask, -jnp.inf, e)
        att = jax.nn.softmax(e, axis=-1)
        att = jnp.where(mask, 0.0, att)
        return jnp.einsum('bij,bjo->bio', att, Wh)

    def _L1_gnn_ref(node_feats, adj_matrix, W, b, a):
        import jax, jax.numpy as jnp
        import numpy as np
        B, N, C_IN, H, C_OUT = (8, 512, 128, 4, 128)
        C = C_OUT // H
        ALPHA = 0.2
        NEG_INF = -9000000000000000.0
        Bb, Nn, _ = node_feats.shape
        Hh, twoC = a.shape
        Cc = twoC // 2
        h = (node_feats @ W.T + b).reshape(Bb, Nn, Hh, Cc)
        a_src, a_dst = (a[:, :Cc], a[:, Cc:])
        l_src = jnp.einsum('bihc,hc->bih', h, a_src)
        l_dst = jnp.einsum('bjhc,hc->bjh', h, a_dst)
        logits = jax.nn.leaky_relu(l_src[:, :, None, :] + l_dst[:, None, :, :], ALPHA)
        logits = jnp.where(adj_matrix[..., None] == 1, logits, NEG_INF)
        probs = jax.nn.softmax(logits, axis=2)
        out = jnp.einsum('bijh,bjhc->bihc', probs, h)
        return out.reshape(Bb, Nn, Hh * Cc)

    def _L2_gnn_ref(hidden, adj, a0, a1, a2, a3, bias):
        import jax, jax.numpy as jnp
        import numpy as np
        B, S, D = (64, 256, 128)

        def _leaky(x):
            return jnp.where(x >= 0, x, 0.2 * x)
        h = hidden

        def e_of(a):
            return _leaky(jnp.einsum('bid,bjd->bij', h * a[:, 0], h))
        e0, e1, e2, e3 = (e_of(a0), e_of(a1), e_of(a2), e_of(a3))
        neg_inf = jnp.float32(-jnp.finfo(e0.dtype).max)
        alpha = jnp.where(adj == 1, e0, neg_inf)
        alpha = jnp.where(adj == 2, e1, alpha)
        alpha = jnp.where(adj == 3, e2, alpha)
        alpha = jnp.where(adj == 4, e3, alpha)
        alpha = jax.nn.sigmoid(alpha)
        return jnp.einsum('bij,bjd->bid', alpha, h) + bias

    def _L3_gnn_ref(x, adj, weight, w_ih, w_hh, b_ih, b_hh):
        import jax, jax.numpy as jnp
        import numpy as np
        OUT = 128
        NUM_LAYERS = 3

        def _gru_cell(inp, h, w_ih, w_hh, b_ih, b_hh):
            gi = inp @ w_ih.T + b_ih
            gh = h @ w_hh.T + b_hh
            i_r, i_z, i_n = jnp.split(gi, 3, axis=-1)
            h_r, h_z, h_n = jnp.split(gh, 3, axis=-1)
            r = jax.nn.sigmoid(i_r + h_r)
            z = jax.nn.sigmoid(i_z + h_z)
            n = jnp.tanh(i_n + r * h_n)
            return (1.0 - z) * n + z * h
        A = (adj != 0).astype(x.dtype)
        h = x
        L = weight.shape[0]
        for i in range(L):
            m = jnp.einsum('bnd,de->bne', h, weight[i])
            aggr = jnp.einsum('bst,bsd->btd', A, m)
            h = _gru_cell(aggr, h, w_ih, w_hh, b_ih, b_hh)
        return h
    h = jnp.maximum(_layernorm(x, axis=-1), 0.0)
    x = x + _L0_gnn_ref(h, adj, L0_gnn_W, L0_gnn_a)
    h = jnp.maximum(_layernorm(x, axis=-1), 0.0)
    x = x + _L1_gnn_ref(h, adj, L1_gnn_W, L1_gnn_b, L1_gnn_a)
    h = jnp.maximum(_layernorm(x, axis=-1), 0.0)
    x = x + _L2_gnn_ref(h, adj, L2_gnn_a0, L2_gnn_a1, L2_gnn_a2, L2_gnn_a3, L2_gnn_bias)
    h = jnp.maximum(_layernorm(x, axis=-1), 0.0)
    x = x + _L3_gnn_ref(h, adj, L3_gnn_weight, L3_gnn_w_ih, L3_gnn_w_hh, L3_gnn_b_ih, L3_gnn_b_hh)
    return x

_drawn_inputs = setup_inputs


def setup_inputs(seed=0):
    import zlib

    import numpy as np

    out = dict(_drawn_inputs(seed))
    spreads = {'L1_gnn_b': (0.0, 0.1), 'L2_gnn_bias': (0.0, 0.295)}
    factors = {'L3_gnn_b_ih': 5.552, 'L3_gnn_b_hh': 8.0}
    for name, (base, spread) in spreads.items():
        noise = np.random.default_rng([zlib.crc32(name.encode()), seed]).standard_normal(out[name].shape)
        drawn = base * np.exp(spread * noise) if base else spread * noise
        out[name] = jnp.asarray(drawn.astype(out[name].dtype))
    for name, factor in factors.items():
        out[name] = (out[name] * factor).astype(out[name].dtype)
    return out
```

```python
from contextlib import ExitStack

import concourse.bass as bass
from concourse import mybir

fp32 = mybir.dt.float32
bf16 = mybir.dt.bfloat16
i32 = mybir.dt.int32
ALU = mybir.AluOpType
ACT = mybir.ActivationFunctionType

P = 128
EPS = 1e-5
SLOPE = 0.2
MASK = 9e15 / SLOPE

PART_AFTER = {0: (0, 0), 2: (0, 1), 4: (0, 2), 6: (0, 3),
              8: (1, 0), 10: (1, 1), 13: (1, 2), 16: (1, 3),
              17: (2, 0), 20: (2, 1), 22: (2, 2), 25: (2, 3)}


class Place:

    def __init__(self, pair, rest):
        self.pair, self.rest = pair, rest

    def count(self, per_graph, within):
        fixed = self.rest * per_graph + within
        return fixed if self.pair is None else self.pair * (2 * per_graph) + fixed

    def count_of_parity(self, per_graph, within):
        fixed = (self.rest // 2) * per_graph + within
        return fixed if self.pair is None else self.pair * per_graph + fixed

    def index(self):
        return self.rest if self.pair is None else self.pair * 2 + self.rest

    def before(self, n=1):
        return Place(self.pair, self.rest - n)

    def exists(self):
        return self.pair is not None or self.rest >= 0


def graph_layers(nc, x, adj, adj_t, w0, w0_t, a0, w1, w1_t, a1, b1, sess_a, b2, gate_w_t, w_ih_t, w_hh_t,
                 b_ih, b_hh, out):
    G, N, D = x.shape
    C = N // P
    H1 = 4
    HD = D // H1
    HEADS = 1 + H1
    UNITS = HEADS * C
    KINDS = 4
    LAYERS = gate_w_t.shape[1]
    LNS = 4

    ctx = ExitStack()
    with ctx:
        def sb(name, shape, dt=fp32):
            return ctx.enter_context(nc.sbuf_tensor(name, shape, dt))

        def sem(name):
            return ctx.enter_context(nc.semaphore(name))

        ident = sb("ident", [P, P])
        ones = sb("ones", [P, P])
        diag = sb("diag", [P, 2, P])
        w0_sb, w0t_sb, a0_sb = sb("w0_sb", [P, D]), sb("w0t_sb", [P, D]), sb("a0_sb", [P, 2])
        w1_sb, w1t_sb, a1_sb = sb("w1_sb", [P, D]), sb("w1t_sb", [P, D]), sb("a1_sb", [P, 2])
        b1_sb, b2_sb, sess_sb = sb("b1_sb", [P, 1]), sb("b2_sb", [P, 1]), sb("sess_sb", [P, KINDS])
        a1_heads = sb("a1_heads", [P, 2, H1])
        b1_rep = sb("b1_rep", [P, P])
        src_w = sb("src_w", [P, HEADS])
        dst_w = sb("dst_w", [P, HEADS])
        dst_rep = sb("dst_rep", [P, HEADS, P])
        head_const = sb("head_const", [P, H1])
        head_parts = sb("head_parts", [P, 2, H1])
        b1_rows, b2_rows = sb("b1_rows", [P, D]), sb("b2_rows", [P, D])
        gate_wt_sb = sb("gate_wt_sb", [P, LAYERS, D])
        w_iht_sb, w_hht_sb = sb("w_iht_sb", [P, 3 * D]), sb("w_hht_sb", [P, 3 * D])
        gi_w = sb("gi_w", [P, LAYERS, 3 * D])
        bih_sb, bhh_sb = sb("bih_sb", [P, 3]), sb("bhh_sb", [P, 3])
        gate_b = sb("gate_b", [P, 3])
        half_bhn = sb("half_bhn", [P, 1])
        ln_const = sb("ln_const", [P, 5, C])

        xin = sb("xin", [P, 2, C, D])
        adj_i = sb("adj_i", [P, C, N], i32)
        adjt_i = sb("adjt_i", [P, C, N], i32)
        mask0, mask1 = sb("mask0", [P, C, N], bf16), sb("mask1", [P, C, N], bf16)
        x1, x1b, x2, x2b = (sb(n, [P, C, D]) for n in ("x1", "x1b", "x2", "x2b"))
        stats = sb("stats", [P, C, 6])
        ln_tmp = sb("ln_tmp", [P, 6, C])
        mean, rstd = sb("mean", [P, C]), sb("rstd", [P, C])
        hn = sb("hn", [P, C, D])
        hT = sb("hT", [P, N])
        values = sb("values", [P, C, D])
        s1 = sb("s1", [P, HEADS, C])
        rmax, negm, den = sb("rmax", [P, HEADS, C]), sb("negm", [P, HEADS, C]), sb("den", [P, HEADS, C])
        mtmp = sb("mtmp", [P, 2, C])
        rden = sb("rden", [P, HEADS, C])
        alive = sb("alive", [P, C])
        probs = sb("probs", [P, 2 * C, N])
        lin = sb("lin", [P, 2, N])
        pT = sb("pT", [P, H1, C, N])
        avT = sb("avT", [P, N])
        scaled = sb("scaled", [P, C, D])
        hTa = sb("hTa", [P, KINDS, N])
        sess = sb("sess", [P, C, N])
        alpha = sb("alpha", [P, C, N])
        kind_mask = sb("kind_mask", [P, N], i32)
        upto = sb("upto", [P, N])
        any_kind = sb("any_kind", [P, C, N])
        settle_cell = sb("settle_cell", [P, 2])

        x3 = sb("x3", [P, 2, C, D])
        edges = sb("edges", [P, 2, C, N])
        h3 = sb("h3", [P, 2, C, D])
        h3T = sb("h3T", [P, 2, N])

        aggT = sb("aggT", [P, N])
        hid_n = sb("hid_n", [P, N])
        r_t, z_t, n_t = sb("r_t", [P, N]), sb("z_t", [P, N]), sb("n_t", [P, N])
        g_tmp, g_diff = sb("g_tmp", [P, N]), sb("g_diff", [P, N])
        hBT = sb("hBT", [P, 2, N])
        hB = sb("hB", [P, C, D])
        out_sb = sb("out_sb", [P, 2, C, D])

        def bank(name):
            return ctx.enter_context(nc.psum_tensor(name, [P, N], fp32))

        dst_bank, turn0, turn1, av_bank = bank("dst_bank"), bank("turn0"), bank("turn1"), bank("av_bank")
        r_bank, z_bank, n_bank, h_bank = bank("r_bank"), bank("z_bank"), bank("n_bank"), bank("h_bank")
        turn = (turn0, turn1)
        z_banks = (dst_bank, turn0, turn1)

        w_loaded = sem("w_loaded")
        const_ready = sem("const_ready")
        w_step = sem("w_step")
        pe_w = sem("pe_w")
        x_loaded = [sem("x_loaded0"), sem("x_loaded1")]
        adj_loaded, adjt_loaded = sem("adj_loaded"), sem("adjt_loaded")
        adj_used, adjt_used = sem("adj_used"), sem("adjt_used")
        stats_ready = sem("stats_ready")
        ln_ready = sem("ln_ready")
        pool_step = sem("pool_step")
        hn_ready = sem("hn_ready")
        hT_ready, hT_copied = sem("hT_ready"), sem("hT_copied")
        val_ready, val_copied = sem("val_ready"), sem("val_copied")
        s1_copied = sem("s1_copied")
        dst_ready, dst_read = sem("dst_ready"), sem("dst_read")
        logits_ready = sem("logits_ready")
        probs_ready = sem("probs_ready")
        turned = sem("turned")
        pT_copied = sem("pT_copied")
        av_done = sem("av_done")
        avT_copied, av_turned = sem("avT_copied"), sem("av_turned")
        res_ready = sem("res_ready")
        bias_added = sem("bias_added")
        hTa_ready = sem("hTa_ready")
        z_ready = sem("z_ready")
        z0_copied = sem("z0_copied")
        zk_used = sem("zk_used")
        sess_ready, tanh_ready = sem("sess_ready"), sem("tanh_ready")
        alpha_ready = sem("alpha_ready")
        dve_a = sem("dve_a")
        gh_ready = sem("gh_ready")
        agg_ready, agg_copied = sem("agg_ready"), sem("agg_copied")
        hid_copied = sem("hid_copied")
        gi_ready = sem("gi_ready")
        gates_ready = sem("gates_ready")
        pre_n_ready, n_ready = sem("pre_n_ready"), sem("n_ready")
        state_ready = sem("state_ready")
        state_turned = sem("state_turned")
        state_copied = sem("state_copied")
        dve_b = sem("dve_b")
        out_ready = sem("out_ready")
        stored = [sem("stored0"), sem("stored1")]

        NA = 91
        PS = 4 * LNS

        block = ctx.enter_context(nc.Block())

        def over_graphs(eng, stage_a, part_b):
            def graph(pa, pb):
                def between(unit):
                    if pb is not None and unit in PART_AFTER:
                        part_b(pb, *PART_AFTER[unit])
                stage_a(pa, between)

            graph(Place(None, 0), None)
            graph(Place(None, 1), Place(None, 0))
            with eng.Fori(1, G // 2) as pair:
                for u in range(2):
                    graph(Place(pair, u), Place(pair, u - 1))
            for unit in sorted(PART_AFTER):
                part_b(Place(None, G - 1), *PART_AFTER[unit])

        LOADS = [(w0_sb, w0), (w0t_sb, w0_t), (a0_sb, a0), (w1_sb, w1), (w1t_sb, w1_t), (a1_sb, a1), (b1_sb, b1),
                 (b2_sb, b2), (gate_wt_sb, gate_w_t), (w_iht_sb, w_ih_t), (w_hht_sb, w_hh_t), (bih_sb, b_ih),
                 (bhh_sb, b_hh)]

        @block.sync
        def _(sp):
            for dst, src in LOADS:
                sp.dma_start(dst[:], src).then_inc(w_loaded, 16)
            for k in range(KINDS):
                sp.dma_start(sess_sb[:, k:k + 1], sess_a[k]).then_inc(w_loaded, 16)

            def rows(array, p):
                return array[bass.ds(p.index(), 1), :, :].rearrange("o (c p) n -> p (o c) n", p=P)

            def stage_a(p, between):
                par = p.rest % 2
                prev, prev2 = p.before(), p.before(2)
                if prev.exists():
                    sp.wait_ge(adj_used, prev.count(1, 1))
                sp.dma_start(adj_i[:], rows(adj, p)).then_inc(adj_loaded, 16)
                if prev2.exists():
                    sp.wait_ge(res_ready, prev2.count(3, 1))
                sp.dma_start(xin[:, par, :, :], rows(x, p)).then_inc(x_loaded[par], 16)
                if prev.exists():
                    sp.wait_ge(adjt_used, prev.count(1, 1))
                sp.dma_start(adjt_i[:], rows(adj_t, p)).then_inc(adjt_loaded, 16)
                for unit in sorted(PART_AFTER):
                    between(unit)

            def part_b(p, layer, part):
                if (layer, part) == (LAYERS - 1, 3):
                    par = p.rest % 2
                    sp.wait_ge(out_ready, p.count(1, 1))
                    sp.dma_start(rows(out, p), out_sb[:, par, :, :]).then_inc(stored[par], 16)

            over_graphs(sp, stage_a, part_b)
            for par in range(2):
                sp.wait_ge(stored[par], 16 * (G // 2))

        @block.gpsimd
        def _(pool):
            g = nc.gpsimd
            g.memset(ones[:], 1.0).then_inc(const_ready, 1)
            g.memset(ident[:], 0.0).then_inc(const_ready, 1)
            for n, value in enumerate((0.5, 0.25, 1.0 / D, EPS, -0.5)):
                g.memset(ln_const[:, n, :], value).then_inc(const_ready, 1)
            pool.wait_ge(const_ready, 7)
            g.affine_select(out=ident[:], in_=ident[:], compare_op=ALU.not_equal, fill=1.0, base=0,
                            pattern=[[-1, P]], channel_multiplier=1).then_inc(const_ready, 1)
            half, quarter, per_d, eps, power = (ln_const[:, n, :] for n in range(5))

            def stage_a(p, between):
                step = [0]

                def own(ins):
                    step[0] += 1
                    ins.then_inc(pool_step, 1)
                    pool.wait_ge(pool_step, p.count(PS, step[0]))

                def norm(n):
                    pool.wait_ge(stats_ready, p.count(LNS, n + 1))
                    me, mo = stats[:, :, 1], stats[:, :, 4]
                    total, gap, within, gap2, base, var = (ln_tmp[:, k, :] for k in range(6))
                    g.tensor_tensor(total, me, mo, op=ALU.add)
                    g.tensor_tensor(within, stats[:, :, 2], stats[:, :, 5], op=ALU.add)
                    own(g.tensor_tensor(gap, me, mo, op=ALU.subtract))
                    g.tensor_tensor(mean[:], total, half, op=ALU.mult)
                    g.tensor_tensor(within, within, per_d, op=ALU.mult)
                    own(g.tensor_tensor(gap2, gap, gap, op=ALU.mult))
                    g.tensor_tensor(base, within, eps, op=ALU.add)
                    own(g.tensor_tensor(gap2, gap2, quarter, op=ALU.mult))
                    own(g.tensor_tensor(var, base, gap2, op=ALU.add))
                    g.tensor_tensor(rstd[:], var, power, op=ALU.pow).then_inc(ln_ready, 1)

                def add_bias(n, dst, src, rows):
                    pool.wait_ge(res_ready, p.count(3, n + 1))
                    g.tensor_tensor(dst[:], src[:], rows[:, :].unsqueeze(1).to_broadcast([P, C, D]),
                                    op=ALU.add).then_inc(bias_added, 1)

                norm(0)
                if p.rest == 0 and p.pair is None:
                    pool.wait_ge(w_step, 13)
                norm_after = {1: (0, x1b, x1, b1_rows), 2: (1, x2b, x2, b2_rows)}
                for n in range(1, LNS):
                    norm(n)
                    if n in norm_after:
                        add_bias(*norm_after[n])
                assert step[0] == PS, step[0]

            over_graphs(pool, stage_a, lambda p, layer, part: None)

        @block.scalar
        def _(act):
            s = nc.scalar

            def copy_turned(p, unit):
                act.wait_ge(turned, p.count(UNITS, unit + 1))
                head, c = divmod(unit, C)
                if head == 1 and c == 0:
                    act.wait_ge(av_done, p.count(3, 1))
                if head == 0 and c == 0 and p.before().exists():
                    act.wait_ge(av_done, p.before().count(3, 2))
                dst = pT[:, max(head - 1, 0), :, c * P:(c + 1) * P]
                s.activation(dst, turn[unit % 2][:, :].rearrange("p (j i) -> p j i", j=C),
                             ACT.Copy).then_inc(pT_copied, 1)

            def copy_hT(p, n):
                act.wait_ge(hT_ready, p.count(LNS, n + 1))
                dst = h3T[:, p.rest % 2, :] if n == LNS - 1 else hT[:, :]
                s.activation(dst, turn0[:, :], ACT.Copy).then_inc(hT_copied, 1)

            def stage_a(p, between):
                def copy_values(n):
                    act.wait_ge(val_ready, p.count(2, n + 1))
                    s.activation(values[:, :, :].rearrange("p c d -> p (c d)"), av_bank[:, :],
                                 ACT.Copy).then_inc(val_copied, 1)

                def exponentials(unit):
                    head, c = divmod(unit, C)
                    act.wait_ge(logits_ready, p.count(UNITS, unit + 1))
                    row = probs[:, (head % 2) * C + c, :]
                    s.activation(row, row, ACT.Exp, bias=negm[:, head, c:c + 1],
                                 accum_out=den[:, head, c:c + 1]).then_inc(probs_ready, 1)

                copy_hT(p, 0)
                copy_values(0)
                between(0)
                for unit in range(C):
                    exponentials(unit)
                    if unit:
                        copy_turned(p, unit - 1)
                    between(1 + unit)
                copy_turned(p, C - 1)
                between(5)
                copy_hT(p, 1)
                copy_values(1)
                between(6)
                for unit in range(C, UNITS):
                    exponentials(unit)
                    if unit > C:
                        copy_turned(p, unit - 1)
                    between(3 + unit)
                copy_turned(p, UNITS - 1)
                act.wait_ge(av_done, p.count(3, 2))
                s.activation(avT[:, :], av_bank[:, :], ACT.Copy).then_inc(avT_copied, 1)
                between(23)
                copy_hT(p, 2)
                for j in range(C):
                    act.wait_ge(z_ready, p.count(KINDS * C, KINDS * j + 1))
                    s.activation(sess[:, j, :], z_banks[KINDS * j % 3][:, :], ACT.Copy).then_inc(z0_copied, 1)
                    if j:
                        tanh_of(p, j - 1)
                    between(24 + j)
                tanh_of(p, C - 1)
                between(28)
                copy_hT(p, 3)
                between(29)

            def tanh_of(p, j):
                act.wait_ge(sess_ready, p.count(C, j + 1))
                s.activation(sess[:, j, :], sess[:, j, :], ACT.Tanh, scale=0.5).then_inc(tanh_ready, 1)

            def part_b(p, layer, part):
                n = layer + 1
                if part == 0:
                    act.wait_ge(gh_ready, p.count(LAYERS, n))
                    s.activation(hid_n[:, :], h_bank[:, :], ACT.Identity, bias=half_bhn[:, 0:1],
                                 scale=0.5).then_inc(hid_copied, 1)
                    act.wait_ge(agg_ready, p.count(LAYERS, n))
                    s.activation(aggT[:, :], n_bank[:, :], ACT.Copy).then_inc(agg_copied, 1)
                elif part == 1:
                    act.wait_ge(gi_ready, p.count(LAYERS, n))
                    s.activation(r_t[:, :], r_bank[:, :], ACT.Tanh, bias=gate_b[:, 0:1], scale=0.5)
                    s.activation(z_t[:, :], z_bank[:, :], ACT.Tanh, bias=gate_b[:, 1:2],
                                 scale=0.5).then_inc(gates_ready, 1)
                elif part == 2:
                    act.wait_ge(pre_n_ready, p.count(LAYERS, n))
                    s.activation(n_t[:, :], g_tmp[:, :], ACT.Tanh, bias=gate_b[:, 2:3]).then_inc(n_ready, 1)
                elif layer < LAYERS - 1:
                    act.wait_ge(state_turned, p.count(LAYERS, n))
                    s.activation(hB[:, :, :].rearrange("p c d -> p (c d)"), h_bank[:, :],
                                 ACT.Copy).then_inc(state_copied, 1)

            act.wait_ge(w_step, 12)
            over_graphs(act, stage_a, part_b)

        @block.vector
        def _(dve):
            v = nc.vector
            wstep = [0]

            def w_own(ins):
                wstep[0] += 1
                ins.then_inc(w_step, 1)
                dve.wait_ge(w_step, wstep[0])

            dve.wait_ge(const_ready, 8)
            dve.wait_ge(w_loaded, 16 * (len(LOADS) + KINDS))
            w_own(v.memset(a1_heads[:, :, :], 0.0))
            for h in range(H1):
                q = slice(h * HD, (h + 1) * HD)
                last = v.tensor_copy(a1_heads[q, :, h], a1_sb[q, :])
            w_own(last)
            w_own(v.tensor_scalar(b1_rep[:], ones[:], b1_sb[:, 0:1], None, ALU.mult))
            v.tensor_scalar(diag[:, 0, :], ident[:], b1_sb[:, 0:1], None, ALU.mult)
            w_own(v.tensor_scalar(diag[:, 1, :], ident[:], b2_sb[:, 0:1], None, ALU.mult))
            v.tensor_tensor(gate_b[:, 0:2], bih_sb[:, 0:2], bhh_sb[:, 0:2], ALU.add)
            v.tensor_copy(gate_b[:, 2:3], bih_sb[:, 2:3])
            w_own(v.tensor_scalar(half_bhn[:], bhh_sb[:, 2:3], 0.5, None, ALU.mult))
            w_own(v.tensor_scalar(gate_b[:, 0:2], gate_b[:, 0:2], 0.5, None, ALU.mult))
            dve.wait_ge(pe_w, 1)
            v.tensor_copy(src_w[:, 0:1], dst_bank[:, 0:1])
            v.tensor_copy(dst_w[:, 0:1], dst_bank[:, 1:2])
            v.tensor_copy(src_w[:, 1:HEADS], dst_bank[:, 2:2 + H1])
            v.tensor_copy(dst_w[:, 1:HEADS], dst_bank[:, 2 + H1:2 + 2 * H1])
            w_own(v.tensor_copy(head_parts[:, :, :].rearrange("p a h -> p (a h)"), dst_bank[:, 16:16 + 2 * H1]))
            for h in range(HEADS):
                last = v.tensor_scalar(dst_rep[:, h, :], ones[:], dst_w[:, h:h + 1], None, ALU.mult)
            w_own(last)
            w_own(v.tensor_tensor(head_const[:], head_parts[:, 0, :], head_parts[:, 1, :], ALU.add))
            dve.wait_ge(pe_w, 2)
            v.tensor_copy(b1_rows[:], av_bank[:, 0:D])
            w_own(v.tensor_copy(b2_rows[:], av_bank[:, D:2 * D]))
            for i, bk in enumerate((r_bank, z_bank, n_bank)):
                dve.wait_ge(pe_w, 3 + i)
                last = v.tensor_copy(gi_w[:, i, :], bk[:, 0:3 * D])
            w_own(last)
            w_own(v.memset(settle_cell[:], 0.0))
            w_own(v.memset(settle_cell[:], 0.0))

            def stage_a(p, between):
                par = p.rest % 2
                step = [0]

                def own(ins):
                    step[0] += 1
                    ins.then_inc(dve_a, 1)
                    dve.wait_ge(dve_a, p.count(NA, step[0]))

                def norm(n, rows):
                    for c in range(C):
                        last = v.bn_stats(stats[:, c, :], rows[:, c, :])
                    last.then_inc(stats_ready, 1)
                    dve.wait_ge(ln_ready, p.count(LNS, n + 1))
                    dst = h3[:, par, :, :] if n == LNS - 1 else hn[:, :, :]
                    if n:
                        dve.wait_ge(hT_ready, p.count(LNS, n))
                    for c in range(C):
                        last = v.tensor_scalar(dst[:, c, :], rows[:, c, :], mean[:, c:c + 1], rstd[:, c:c + 1],
                                               ALU.subtract, ALU.mult)
                    own(last)
                    v.tensor_scalar(dst, dst, 0.0, None, ALU.max).then_inc(hn_ready, 1)

                def masked_max(head, c):
                    masks = mask0 if head == 0 else mask1
                    v.tensor_tensor_reduce(out=probs[:, (head % 2) * C + c, :], in0=dst_bank[:, :],
                                           in1=masks[:, c, :], scale=1.0, scalar=-3e38, op0=ALU.add, op1=ALU.max,
                                           accum_out=rmax[:, head, c:c + 1])

                def settle():
                    dve.wait_ge(dve_a, p.count(NA, step[0]))
                    step[0] += 1
                    v.memset(settle_cell[:, 0:1], 0.0).then_inc(dve_a, 1)

                def next_max(head, c):
                    if c == 0:
                        dve.wait_ge(dst_ready, p.count(HEADS, head + 1))
                    if head >= 2:
                        dve.wait_ge(turned, p.count(UNITS, (head - 2) * C + c + 1))
                    elif p.before().exists():
                        back = (HEADS - 1 if head == 0 else HEADS - 2) * C
                        dve.wait_ge(turned, p.before().count(UNITS, back + c + 1))
                    settle()
                    masked_max(head, c)

                def negative_max(head):
                    own(v.memset(settle_cell[:, 1:2], 0.0))
                    own(v.tensor_tensor(mtmp[:, 0, :], rmax[:, head, :], s1[:, head, :], ALU.add))
                    own(v.tensor_scalar(mtmp[:, 1, :], mtmp[:, 0, :], -SLOPE, None, ALU.mult))
                    v.scalar_tensor_tensor(negm[:, head, :], mtmp[:, 0, :], -1.0, mtmp[:, 1, :], ALU.mult,
                                           ALU.min).then_inc(dst_read, 1)

                def logits(head, c):
                    row = probs[:, (head % 2) * C + c, :]
                    own(v.tensor_scalar(lin[:, c % 2, :], row, s1[:, head, c:c + 1], SLOPE, ALU.add, ALU.mult))
                    v.scalar_tensor_tensor(row, row, s1[:, head, c:c + 1], lin[:, c % 2, :], ALU.add,
                                           ALU.max).then_inc(logits_ready, 1)

                dve.wait_ge(adj_loaded, p.count(16, 16))
                v.tensor_scalar(mask0[:, :, :], adj_i[:, :, :], 0.0, -MASK, ALU.is_equal, ALU.mult)
                dve.wait_ge(x_loaded[par], p.count_of_parity(16, 16))
                norm(0, xin[:, par, :, :])
                v.tensor_scalar(mask1[:, :, :], adj_i[:, :, :], 1.0, -MASK, ALU.not_equal, ALU.mult)
                dve.wait_ge(val_ready, p.count(2, 1))
                v.tensor_copy(s1[:, 0, :], turn1[:, 0:C]).then_inc(s1_copied, 1)
                for c in range(C):
                    next_max(0, c)
                negative_max(0)
                v.tensor_scalar(edges[:, par, :, :], adj_i[:, :, :], 0.0, 1.0, ALU.not_equal,
                                ALU.mult).then_inc(adj_used, 1)
                between(0)
                for c in range(C):
                    logits(0, c)
                    between(1 + c)
                dve.wait_ge(probs_ready, p.count(UNITS, C))
                v.tensor_scalar(alive[:, :], rmax[:, 0, :], -MASK / 2, None, ALU.is_gt)
                own(v.reciprocal(rden[:, 0, :], den[:, 0, :]))
                own(v.tensor_tensor(rden[:, 0, :], rden[:, 0, :], alive[:, :], ALU.mult))
                dve.wait_ge(av_done, p.count(3, 1))
                for c in range(C):
                    last = v.scalar_tensor_tensor(x1[:, c, :], av_bank[:, c * P:(c + 1) * P], rden[:, 0, c:c + 1],
                                                  xin[:, par, c, :], ALU.mult, ALU.add)
                last.then_inc(res_ready, 1)
                dve.wait_ge(res_ready, p.count(3, 1))
                between(5)
                norm(1, x1[:, :, :])
                dve.wait_ge(val_ready, p.count(2, 2))
                v.tensor_tensor(s1[:, 1:HEADS, :], turn1[:, 0:C * H1].rearrange("p (c h) -> p h c", h=H1),
                                head_const[:, :].unsqueeze(2).to_broadcast([P, H1, C]),
                                ALU.add).then_inc(s1_copied, 1)
                for c in range(C):
                    next_max(1, c)
                negative_max(1)
                between(6)
                for head in range(1, HEADS):
                    for c in range(C):
                        logits(head, c)
                        if head < HEADS - 1:
                            next_max(head + 1, c)
                            if c == C - 1:
                                negative_max(head + 1)
                        between(3 + head * C + c)
                dve.wait_ge(probs_ready, p.count(UNITS, UNITS))
                own(v.reciprocal(rden[:, 1:HEADS, :], den[:, 1:HEADS, :]))
                dve.wait_ge(av_turned, p.count(1, 1))
                own(v.tensor_tensor(scaled[:, :, :].rearrange("p c (h e) -> p c h e", h=H1),
                                    turn0[:, :].rearrange("p (c h e) -> p c h e", c=C, h=H1),
                                    rden[:, 1:HEADS, :].rearrange("p h c -> p c h").unsqueeze(3)
                                    .to_broadcast([P, C, H1, HD]), ALU.mult))
                dve.wait_ge(bias_added, p.count(2, 1))
                v.tensor_tensor(x2[:, :, :], x1b[:, :, :], scaled[:, :, :], ALU.add).then_inc(res_ready, 1)
                dve.wait_ge(res_ready, p.count(3, 2))
                between(23)
                norm(2, x2[:, :, :])
                dve.wait_ge(hT_copied, p.count(LNS, 3))
                for k in range(KINDS):
                    last = v.tensor_scalar(hTa[:, k, :], hT[:, :], sess_sb[:, k:k + 1], None, ALU.mult)
                last.then_inc(hTa_ready, 1)
                dve.wait_ge(adjt_loaded, p.count(16, 16))

                def weights_of(j):
                    dve.wait_ge(tanh_ready, p.count(C, j + 1))
                    v.scalar_tensor_tensor(alpha[:, j, :], sess[:, j, :], 1.0, any_kind[:, j, :], ALU.add,
                                           ALU.mult).then_inc(alpha_ready, 1)

                for j in range(C):
                    own(v.tensor_scalar(upto[:, :], adjt_i[:, j, :], float(KINDS), 0.5, ALU.is_le, ALU.mult))
                    v.scalar_tensor_tensor(any_kind[:, j, :], adjt_i[:, j, :], 1.0, upto[:, :], ALU.is_ge, ALU.mult)
                    dve.wait_ge(z0_copied, p.count(C, j + 1))
                    for k in range(1, KINDS):
                        last = v.tensor_scalar(kind_mask[:, :], adjt_i[:, j, :], float(k + 1), None, ALU.is_equal)
                        own(last)
                        n = KINDS * j + k
                        dve.wait_ge(z_ready, p.count(KINDS * C, n + 1))
                        settle()
                        v.copy_predicated(sess[:, j, :], kind_mask[:, :], z_banks[n % 3][:, :]).then_inc(zk_used, 1)
                        dve.wait_ge(zk_used, p.count((KINDS - 1) * C, (KINDS - 1) * j + k))
                    v.scalar_tensor_tensor(sess[:, j, :], sess[:, j, :], SLOPE, sess[:, j, :], ALU.mult,
                                           ALU.max).then_inc(sess_ready, 1)
                    if j:
                        weights_of(j - 1)
                    between(24 + j)
                v.memset(settle_cell[:, 1:2], 0.0).then_inc(adjt_used, 1)
                weights_of(C - 1)
                dve.wait_ge(bias_added, p.count(2, 2))
                dve.wait_ge(av_done, p.count(3, 3))
                v.tensor_tensor(x3[:, par, :, :], av_bank[:, :].rearrange("p (c d) -> p c d", c=C), x2b[:, :, :],
                                ALU.add).then_inc(res_ready, 1)
                dve.wait_ge(res_ready, p.count(3, 3))
                between(28)
                norm(3, x3[:, par, :, :])
                between(29)
                assert step[0] == NA, step[0]

            def part_b(p, layer, part):
                par = p.rest % 2
                n = layer + 1
                prev = h3T[:, par, :] if layer == 0 else hBT[:, (layer + 1) % 2, :]
                new = hBT[:, layer % 2, :]
                first = p.count(4 * LAYERS, 4 * layer)
                if part == 1:
                    dve.wait_ge(hid_copied, p.count(LAYERS, n))
                    dve.wait_ge(gates_ready, p.count(LAYERS, n))
                    v.scalar_tensor_tensor(g_tmp[:, :], r_t[:, :], 1.0, hid_n[:, :], ALU.add,
                                           ALU.mult).then_inc(dve_b, 1)
                    dve.wait_ge(dve_b, p.count(3 * LAYERS, 3 * layer + 1))
                    v.tensor_tensor(g_tmp[:, :], g_tmp[:, :], n_bank[:, :], ALU.add).then_inc(pre_n_ready, 1)
                elif part == 2:
                    dve.wait_ge(n_ready, p.count(LAYERS, n))
                    v.tensor_tensor(g_diff[:, :], prev, n_t[:, :], ALU.subtract).then_inc(dve_b, 1)
                    dve.wait_ge(dve_b, p.count(3 * LAYERS, 3 * layer + 2))
                    v.scalar_tensor_tensor(g_diff[:, :], z_t[:, :], 1.0, g_diff[:, :], ALU.add,
                                           ALU.mult).then_inc(dve_b, 1)
                    dve.wait_ge(dve_b, p.count(3 * LAYERS, 3 * layer + 3))
                    v.scalar_tensor_tensor(new, g_diff[:, :], 0.5, n_t[:, :], ALU.mult,
                                           ALU.add).then_inc(state_ready, 1)
                elif part == 3 and layer == LAYERS - 1:
                    dve.wait_ge(state_turned, p.count(LAYERS, n))
                    prev2 = p.before(2)
                    if prev2.exists():
                        dve.wait_ge(stored[par], prev2.count_of_parity(16, 16))
                    v.tensor_tensor(out_sb[:, par, :, :], h_bank[:, :].rearrange("p (c d) -> p c d", c=C),
                                    x3[:, par, :, :], ALU.add).then_inc(out_ready, 1)

            over_graphs(dve, stage_a, part_b)

        @block.tensor
        def _(pe):
            t = nc.tensor
            pe.wait_ge(w_loaded, 16 * (len(LOADS) + KINDS))
            pe.wait_ge(const_ready, 8)
            pe.wait_ge(w_step, 4)
            t.matmul(dst_bank[:, 0:2], w0_sb[:], a0_sb[:], start=True, stop=True)
            heads_a = a1_heads[:, :, :].rearrange("p a h -> p (a h)")
            t.matmul(dst_bank[:, 2:2 + 2 * H1], w1_sb[:], heads_a, start=True, stop=True)
            t.matmul(dst_bank[:, 16:16 + 2 * H1], b1_rep[:], heads_a, start=True, stop=True).then_inc(pe_w, 1)
            t.matmul(av_bank[:, 0:D], ones[:], diag[:, 0, :], start=True, stop=True)
            t.matmul(av_bank[:, D:2 * D], ones[:], diag[:, 1, :], start=True, stop=True).then_inc(pe_w, 1)
            for i, bk in enumerate((r_bank, z_bank, n_bank)):
                t.matmul(bk[:, 0:3 * D], gate_wt_sb[:, i, :], w_iht_sb[:], start=True, stop=True).then_inc(pe_w, 1)

            def stage_a(p, between):
                prev = p.before()

                def turn_rows(n, rows):
                    pe.wait_ge(hn_ready, p.count(LNS, n + 1))
                    if n == 0 and prev.exists():
                        pe.wait_ge(hT_copied, prev.count(LNS, LNS))
                    if n == 1:
                        pe.wait_ge(pT_copied, p.count(UNITS, C))
                    for c in range(C):
                        last = t.transpose(turn0[:, c * P:(c + 1) * P], rows[:, c, :], ident[:])
                    last.then_inc(hT_ready, 1)

                def spread(head):
                    if head >= 1:
                        pe.wait_ge(dst_read, p.count(HEADS, head))
                    t.matmul(dst_bank[:, :], dst_rep[:, head, :], hT[:, :], start=True,
                             stop=True).then_inc(dst_ready, 1)

                def project(n, wt, src, heads):
                    pe.wait_ge(hT_copied, p.count(LNS, n + 1))
                    if n == 1:
                        pe.wait_ge(res_ready, p.count(3, 1))
                    elif prev.exists():
                        pe.wait_ge(res_ready, prev.count(3, 3))
                    for c in range(C):
                        t.matmul(turn1[:, c * heads:(c + 1) * heads], hT[:, c * P:(c + 1) * P], src, start=True,
                                 stop=True)
                    for c in range(C):
                        last = t.matmul(av_bank[:, c * P:(c + 1) * P], hT[:, c * P:(c + 1) * P], wt, start=True,
                                        stop=True)
                    last.then_inc(val_ready, 1)

                def turn_probs(unit):
                    head, c = divmod(unit, C)
                    pe.wait_ge(probs_ready, p.count(UNITS, unit + 1))
                    if unit in (0, C):
                        pe.wait_ge(s1_copied, p.count(2, 1 + unit // C))
                    if unit >= 2:
                        pe.wait_ge(pT_copied, p.count(UNITS, unit - 1))
                    for j in range(C):
                        last = t.transpose(turn[unit % 2][:, j * P:(j + 1) * P],
                                           probs[:, (head % 2) * C + c, j * P:(j + 1) * P], ident[:])
                    last.then_inc(turned, 1)

                def sum_l0(c):
                    pe.wait_ge(pT_copied, p.count(UNITS, c + 1))
                    if c == 0:
                        pe.wait_ge(val_copied, p.count(2, 1))
                    for j in range(C):
                        last = t.matmul(av_bank[:, c * P:(c + 1) * P], pT[:, 0, j, c * P:(c + 1) * P],
                                        values[:, j, :], start=(j == 0), stop=(j == C - 1))
                    return last

                turn_rows(0, hn)
                project(0, w0t_sb[:], src_w[:, 0:1], 1)
                spread(0)
                between(0)
                for c in range(C):
                    turn_probs(c)
                    if c:
                        sum_l0(c - 1)
                    between(1 + c)
                sum_l0(C - 1).then_inc(av_done, 1)
                between(5)
                turn_rows(1, hn)
                project(1, w1t_sb[:], src_w[:, 1:HEADS], H1)
                spread(1)
                between(6)
                for unit in range(C, UNITS):
                    head, c = divmod(unit, C)
                    if c == 0 and head < HEADS - 1:
                        spread(head + 1)
                    turn_probs(unit)
                    between(3 + unit)
                pe.wait_ge(pT_copied, p.count(UNITS, UNITS))
                pe.wait_ge(val_copied, p.count(2, 2))
                for j in range(C):
                    for h in range(H1):
                        last = t.matmul(av_bank[h * HD:(h + 1) * HD, :], values[:, j, h * HD:(h + 1) * HD],
                                        pT[:, h, j, :], start=(j == 0), stop=(j == C - 1), skip_group_check=True)
                last.then_inc(av_done, 1)
                pe.wait_ge(avT_copied, p.count(1, 1))
                for c in range(C):
                    last = t.transpose(turn0[:, c * P:(c + 1) * P], avT[:, c * P:(c + 1) * P], ident[:])
                last.then_inc(av_turned, 1)
                between(23)
                turn_rows(2, hn)
                pe.wait_ge(hTa_ready, p.count(1, 1))
                for j in range(C):
                    for k in range(KINDS):
                        n = KINDS * j + k
                        if n >= 3:
                            bj, bk = divmod(n - 3, KINDS)
                            if bk == 0:
                                pe.wait_ge(z0_copied, p.count(C, bj + 1))
                            else:
                                pe.wait_ge(zk_used, p.count((KINDS - 1) * C, (KINDS - 1) * bj + bk))
                        t.matmul(z_banks[n % 3][:, :], hT[:, j * P:(j + 1) * P], hTa[:, k, :], start=True,
                                 stop=True).then_inc(z_ready, 1)
                    between(24 + j)
                pe.wait_ge(alpha_ready, p.count(C, C))
                for c in range(C):
                    for j in range(C):
                        last = t.matmul(av_bank[:, c * P:(c + 1) * P], alpha[:, j, c * P:(c + 1) * P], hn[:, j, :],
                                        start=(j == 0), stop=(j == C - 1))
                last.then_inc(av_done, 1)
                between(28)
                turn_rows(3, h3[:, p.rest % 2, :, :])
                between(29)

            def part_b(p, layer, part):
                par = p.rest % 2
                n = layer + 1
                stateT = h3T[:, par, :] if layer == 0 else hBT[:, (layer + 1) % 2, :]
                state = h3[:, par, :, :] if layer == 0 else hB[:, :, :]
                prev = p.before()
                if part == 0:
                    if layer == 0:
                        pe.wait_ge(hT_copied, p.count(LNS, LNS))
                        if prev.exists():
                            pe.wait_ge(out_ready, prev.count(1, 1))
                    else:
                        pe.wait_ge(state_copied, p.count(LAYERS - 1, layer))
                    t.matmul(h_bank[:, :], w_hht_sb[:, 2 * D:3 * D], stateT, start=True, stop=True)\
                        .then_inc(gh_ready, 1)
                    for s in range(C):
                        last = t.matmul(n_bank[:, :], state[:, s, :], edges[:, par, s, :], start=(s == 0),
                                        stop=(s == C - 1))
                    last.then_inc(agg_ready, 1)
                    t.matmul(r_bank[:, :], w_hht_sb[:, 0:D], stateT, start=True, stop=False)
                    t.matmul(z_bank[:, :], w_hht_sb[:, D:2 * D], stateT, start=True, stop=False)
                elif part == 1:
                    pe.wait_ge(agg_copied, p.count(LAYERS, n))
                    t.matmul(r_bank[:, :], gi_w[:, layer, 0:D], aggT[:, :], start=False, stop=True)
                    t.matmul(z_bank[:, :], gi_w[:, layer, D:2 * D], aggT[:, :], start=False, stop=True)
                    t.matmul(n_bank[:, :], gi_w[:, layer, 2 * D:3 * D], aggT[:, :], start=True, stop=True)\
                        .then_inc(gi_ready, 1)
                elif part == 3:
                    pe.wait_ge(state_ready, p.count(LAYERS, n))
                    new = hBT[:, layer % 2, :]
                    for c in range(C):
                        last = t.transpose(h_bank[:, c * P:(c + 1) * P], new[:, c * P:(c + 1) * P], ident[:])
                    last.then_inc(state_turned, 1)

            pe.wait_ge(w_step, 12)
            over_graphs(pe, stage_a, part_b)


def kernel(x, adj, L0_gnn_W, L0_gnn_a, L1_gnn_W, L1_gnn_b, L1_gnn_a, L2_gnn_a0, L2_gnn_a1, L2_gnn_a2, L2_gnn_a3,
           L2_gnn_bias, L3_gnn_weight, L3_gnn_w_ih, L3_gnn_w_hh, L3_gnn_b_ih, L3_gnn_b_hh):
    import numpy as np
    import concourse.bacc as bacc
    from concourse.bass_utils import run_bass_kernel_spmd as run

    D = x.shape[-1]
    H1 = L1_gnn_a.shape[0]
    col = lambda a: np.asarray(a).reshape(D, 1)
    laid = {
        "x": x, "adj": adj, "adj_t": np.asarray(adj).swapaxes(1, 2),
        "w0": L0_gnn_W, "w0_t": np.asarray(L0_gnn_W).T, "a0": np.asarray(L0_gnn_a).reshape(2, D).T,
        "w1": L1_gnn_W, "w1_t": np.asarray(L1_gnn_W).T,
        "a1": np.asarray(L1_gnn_a).reshape(H1, 2, D // H1).transpose(0, 2, 1).reshape(D, 2),
        "b1": col(L1_gnn_b),
        "s0": col(L2_gnn_a0), "s1": col(L2_gnn_a1), "s2": col(L2_gnn_a2), "s3": col(L2_gnn_a3),
        "b2": col(L2_gnn_bias),
        "gate_w_t": np.asarray(L3_gnn_weight).transpose(2, 0, 1),
        "w_ih_t": np.asarray(L3_gnn_w_ih).T, "w_hh_t": np.asarray(L3_gnn_w_hh).T,
        "b_ih": np.asarray(L3_gnn_b_ih).reshape(3, D).T, "b_hh": np.asarray(L3_gnn_b_hh).reshape(3, D).T,
    }
    nc = bacc.Bacc("TRN2", target_bir_lowering=False, num_devices=1)
    arrays, aps = {}, {}
    for name, a in laid.items():
        a = np.ascontiguousarray(a)
        arrays[f"in_{name}"] = a
        aps[name] = nc.dram_tensor(f"in_{name}", a.shape, mybir.dt.from_np(a.dtype), kind="ExternalInput").ap()
    sess_a = [aps.pop(f"s{k}") for k in range(4)]
    out = nc.dram_tensor("out_0", x.shape, mybir.dt.float32, kind="ExternalOutput").ap()
    graph_layers(nc, **aps, sess_a=sess_a, out=out)
    return run(nc, [arrays], core_ids=[0]).results[0]["out_0"]
```

```python
from contextlib import ExitStack

import concourse.bass as bass
from concourse import mybir

fp32 = mybir.dt.float32
bf16 = mybir.dt.bfloat16
i32 = mybir.dt.int32
ALU = mybir.AluOpType
ACT = mybir.ActivationFunctionType
AX = mybir.AxisListType

P = 128
EPS = 1e-5
SLOPE = 0.2
MASK = 2.0 ** 56

A_STEPS = (["stats0", "rows0", "mask0", "mask1", "dst0", "values0"] + [f"m{c}" for c in range(4)]
           + [f"{s}{n}" for n in range(4) for s in "uv"]
           + ["edges", "turned0", "x1", "stats1", "rows1", "dst1", "values1"] + [f"n{c}" for c in range(4)]
           + [f"{s}{n}" for n in range(4, 20) for s in "uv"] + ["turned1", "sum1", "others", "x2"])
B_STEPS = (["stats2", "rows2", "features", "mask2"] + [f"z{n}" for n in range(4)] + ["kinds"]
           + [f"s{n}" for n in range(4)] + [f"w{n}" for n in range(4)] + ["x3", "stats3", "rows3"]
           + [f"g{layer}{part}" for layer in range(3) for part in range(8)])
PLACES = {
    "tensor": (0, 0, 1, 1, 1, 1, 2, 4, 4, 4, 4, 4, 7, 7, 9, 9, 9, 11, 15, 21, 21, 21, 21, 22, 23, 24, 25, 28, 28,
               31, 37, 38, 38, 41, 44, 44, 44, 46, 49, 57, 62, 63, 65, 65,),
    "vector": (0, 0, 1, 1, 1, 1, 3, 4, 4, 4, 4, 4, 5, 5, 5, 8, 8, 14, 17, 17, 17, 17, 17, 23, 23, 24, 26, 30, 39,
               39, 39, 43, 43, 44, 50, 50, 54, 55, 55, 62, 63, 63, 65, 65,),
    "scalar": (0, 0, 0, 0, 1, 1, 2, 3, 4, 4, 4, 4, 4, 6, 6, 18, 18, 20, 20, 20, 20, 20, 21, 22, 23, 23, 26, 30,
               30, 34, 40, 41, 42, 43, 46, 49, 50, 55, 62, 62, 62, 62, 65, 65,),
}
PLACES["gpsimd"] = PLACES["vector"]


def merged(engine):
    order = []
    for n in range(len(A_STEPS) + 1):
        order += [("B", step) for step, place in zip(B_STEPS, PLACES[engine]) if place == n]
        order += [("A", step) for step in A_STEPS[n:n + 1]]
    return order


class Place:

    def __init__(self, pair, rest):
        self.pair, self.rest = pair, rest

    def count(self, per_graph, within):
        fixed = self.rest * per_graph + within
        return fixed if self.pair is None else self.pair * (2 * per_graph) + fixed

    def count_of_parity(self, per_graph, within):
        fixed = (self.rest // 2) * per_graph + within
        return fixed if self.pair is None else self.pair * per_graph + fixed

    def index(self):
        return self.rest if self.pair is None else self.pair * 2 + self.rest

    def before(self, n=1):
        return Place(self.pair, self.rest - n)

    def exists(self):
        return self.pair is not None or self.rest >= 0


def graph_layers(nc, x, adj, adj_t, w0, w0_t, a0, w1, w1_t, a1, b1, sess_a, b2, gate_w_t, w_ih_t, w_hh_t,
                 b_ih, b_hh, out):
    G, N, D = x.shape
    C = N // P
    H1 = 4
    HD = D // H1
    HEADS = 1 + H1
    UNITS = HEADS * C
    KINDS = 4
    LAYERS = gate_w_t.shape[1]
    REST = KINDS - 1

    ctx = ExitStack()
    with ctx:
        def sb(name, shape, dt=fp32):
            return ctx.enter_context(nc.sbuf_tensor(name, shape, dt))

        def sem(name):
            return ctx.enter_context(nc.semaphore(name))

        ident = sb("ident", [P, P])
        ones = sb("ones", [P, P])
        diag = sb("diag", [P, 2, P])
        w0_sb, w0t_sb, a0_sb = sb("w0_sb", [P, D]), sb("w0t_sb", [P, D]), sb("a0_sb", [P, 2])
        w1_sb, w1t_sb, a1_sb = sb("w1_sb", [P, D]), sb("w1t_sb", [P, D]), sb("a1_sb", [P, 2])
        b1_sb, b2_sb, sess_sb = sb("b1_sb", [P, 1]), sb("b2_sb", [P, 1]), sb("sess_sb", [P, KINDS])
        a1_heads = sb("a1_heads", [P, 2, H1])
        b1_rep = sb("b1_rep", [P, P])
        src_w = sb("src_w", [P, HEADS])
        dst_w = sb("dst_w", [P, HEADS])
        dst_rep = sb("dst_rep", [P, HEADS, P])
        head_const = sb("head_const", [P, H1])
        head_parts = sb("head_parts", [P, 2, H1])
        b1_rows, b2_rows = sb("b1_rows", [P, D]), sb("b2_rows", [P, D])
        gate_wt_sb = sb("gate_wt_sb", [P, LAYERS, D])
        w_iht_sb, w_hht_sb = sb("w_iht_sb", [P, 3 * D]), sb("w_hht_sb", [P, 3 * D])
        gi_w = sb("gi_w", [P, LAYERS, 3 * D])
        bih_sb, bhh_sb = sb("bih_sb", [P, 3]), sb("bhh_sb", [P, 3])
        gate_b = sb("gate_b", [P, 3])
        half_bhn = sb("half_bhn", [P, 1])

        xin = sb("xin", [P, 2, C, D])
        adj_i = sb("adj_i", [P, C, N], i32)
        adjt_i = sb("adjt_i", [P, C, N], i32)
        mask0, mask1 = sb("mask0", [P, C, N], bf16), sb("mask1", [P, C, N], bf16)
        x1, x1b = sb("x1", [P, C, D]), sb("x1b", [P, C, D])
        stats = [sb(f"stats{n}", [P, C, 6]) for n in range(2)]
        moments = [sb(f"moments{n}", [P, C, 2]) for n in range(2)]
        var_eps, rstd = ([sb(f"{m}{n}", [P, C]) for n in range(2)] for m in ("var_eps", "rstd"))
        power = sb("power", [P, C])
        hn = [sb(f"hn{n}", [P, C, D]) for n in range(2)]
        hT = [sb(f"hT{n}", [P, N]) for n in range(2)]
        values = sb("values", [P, C, D])
        s1, s1_part = sb("s1", [P, HEADS, C]), sb("s1_part", [P, HEADS, C])
        rmax, negm, den = sb("rmax", [P, HEADS, C]), sb("negm", [P, HEADS, C]), sb("den", [P, HEADS, C])
        mtmp = sb("mtmp", [P, 2, C])
        rden = sb("rden", [P, HEADS, C])
        alive = sb("alive", [P, C])
        probs = sb("probs", [P, 2 * C, N])
        lin = sb("lin", [P, 2, N])
        pT = sb("pT", [P, H1, C, N])
        avT = sb("avT", [P, N])
        scaled = sb("scaled", [P, C, D])
        settle_a, settle_b = sb("settle_a", [P, 4]), sb("settle_b", [P, 4])
        count_w = sb("count_w", [P, 2, P], bf16)

        x2 = sb("x2", [P, 2, C, D])
        edges = sb("edges", [P, 2, C, N])
        other_kinds = sb("other_kinds", [P, 2], i32)

        x2b, x3 = sb("x2b", [P, C, D]), sb("x3", [P, C, D])
        hTa = sb("hTa", [P, KINDS, N])
        sess = sb("sess", [P, C, N])
        alpha = sb("alpha", [P, C, N])
        kind_mask = sb("kind_mask", [P, N], i32)
        upto = sb("upto", [P, N])
        any_kind = sb("any_kind", [P, C, N])
        h3 = sb("h3", [P, C, D])
        h3T = sb("h3T", [P, N])
        aggT = sb("aggT", [P, N])
        hid_n = sb("hid_n", [P, N])
        r_t, z_t, n_t = sb("r_t", [P, N]), sb("z_t", [P, N]), sb("n_t", [P, N])
        g_tmp, g_keep = sb("g_tmp", [P, N]), sb("g_keep", [P, N])
        half_state = sb("half_state", [P, N])
        hBT = sb("hBT", [P, 2, N])
        hB = sb("hB", [P, C, D])
        out_sb = sb("out_sb", [P, 2, C, D])

        def bank(name):
            return ctx.enter_context(nc.psum_tensor(name, [P, N], fp32))

        dst_bank, turn0, turn1, av_bank = bank("dst_bank"), bank("turn0"), bank("turn1"), bank("av_bank")
        r_bank, z_bank, n_bank, h_bank = bank("r_bank"), bank("z_bank"), bank("n_bank"), bank("h_bank")
        turn = (turn0, turn1)
        z_banks = (r_bank, z_bank, n_bank, h_bank)

        w_loaded = sem("w_loaded")
        const_ready = sem("const_ready")
        w_step = sem("w_step")
        pe_w = sem("pe_w")
        x_loaded = [sem("x_loaded0"), sem("x_loaded1")]
        adj_loaded, adjt_loaded = sem("adj_loaded"), sem("adjt_loaded")
        adj_used, adjt_used = sem("adj_used"), sem("adjt_used")
        stats_ready = [sem(f"stats_ready{n}") for n in range(2)]
        ln_ready = [sem(f"ln_ready{n}") for n in range(2)]
        hn_ready = [sem(f"hn_ready{n}") for n in range(2)]
        hT_ready = [sem(f"hT_ready{n}") for n in range(2)]
        hT_copied = [sem(f"hT_copied{n}") for n in range(2)]
        val_ready, val_copied = sem("val_ready"), sem("val_copied")
        s1_copied = sem("s1_copied")
        dst_ready, dst_read = sem("dst_ready"), sem("dst_read")
        small_ready = sem("small_ready")
        logits_ready = sem("logits_ready")
        probs_ready = sem("probs_ready")
        turned = sem("turned")
        pT_copied = sem("pT_copied")
        av_done = sem("av_done")
        avT_copied, av_turned = sem("avT_copied"), sem("av_turned")
        x1_ready, x2_ready = sem("x1_ready"), sem("x2_ready")
        x1b_ready = sem("x1b_ready")
        others_counted, others_ready = sem("others_counted"), sem("others_ready")
        dve_a = sem("dve_a")
        x2b_ready = sem("x2b_ready")
        hTa_ready, hTk_ready = sem("hTa_ready"), sem("hTk_ready")
        z_ready, z_copied = sem("z_ready"), sem("z_copied")
        zk_ready, zk_used = sem("zk_ready"), sem("zk_used")
        dve_k = sem("dve_k")
        sess_ready, tanh_ready = sem("sess_ready"), sem("tanh_ready")
        alpha_ready = sem("alpha_ready")
        av2_done, x3_ready = sem("av2_done"), sem("x3_ready")
        gh_ready = sem("gh_ready")
        agg_ready, agg_copied = sem("agg_ready"), sem("agg_copied")
        hid_copied = sem("hid_copied")
        half_ready = sem("half_ready")
        gi_ready = sem("gi_ready")
        gates_ready = sem("gates_ready")
        pre_n_ready, n_ready = sem("pre_n_ready"), sem("n_ready")
        state_ready = sem("state_ready")
        state_turned = sem("state_turned")
        state_copied = sem("state_copied")
        dve_b = sem("dve_b")
        out_ready = sem("out_ready")
        stored = [sem("stored0"), sem("stored1")]

        S_STEPS = tuple(f"s{n}" for n in range(C))
        NA = 59
        NB = 16
        NK = 29

        block = ctx.enter_context(nc.Block())

        def over_graphs(eng, engine, step_a, step_b):
            for step in A_STEPS:
                step_a(Place(None, 0), step)

            def both(pa, pb):
                for stage, step in merged(engine):
                    if stage == "A":
                        step_a(pa, step)
                    else:
                        step_b(pb, step)

            both(Place(None, 1), Place(None, 0))
            with eng.Fori(1, G // 2) as pair:
                for u in range(2):
                    both(Place(pair, u), Place(pair, u - 1))
            for step in B_STEPS:
                step_b(Place(None, G - 1), step)

        LOADS = [(w0_sb, w0), (w0t_sb, w0_t), (a0_sb, a0), (w1_sb, w1), (w1t_sb, w1_t), (a1_sb, a1), (b1_sb, b1),
                 (b2_sb, b2), (gate_wt_sb, gate_w_t), (w_iht_sb, w_ih_t), (w_hht_sb, w_hh_t), (bih_sb, b_ih),
                 (bhh_sb, b_hh)]

        @block.sync
        def _(sp):
            for dst, src in LOADS:
                sp.dma_start(dst[:], src).then_inc(w_loaded, 16)
            for k in range(KINDS):
                sp.dma_start(sess_sb[:, k:k + 1], sess_a[k]).then_inc(w_loaded, 16)

            def rows(array, p):
                return array[bass.ds(p.index(), 1), :, :].rearrange("o (c p) n -> p (o c) n", p=P)

            def load(p):
                par = p.rest % 2
                prev, prev2 = p.before(), p.before(2)
                if prev.exists():
                    sp.wait_ge(adj_used, prev.count(1, 1))
                sp.dma_start(adj_i[:], rows(adj, p)).then_inc(adj_loaded, 16)
                if prev2.exists():
                    sp.wait_ge(x1_ready, prev2.count(1, 1))
                sp.dma_start(xin[:, par, :, :], rows(x, p)).then_inc(x_loaded[par], 16)

            def load_turned(p):
                if p.before().exists():
                    sp.wait_ge(adjt_used, p.before().count(1, 1))
                sp.dma_start(adjt_i[:], rows(adj_t, p)).then_inc(adjt_loaded, 16)

            def store(p):
                sp.wait_ge(out_ready, p.count(1, 1))
                sp.dma_start(rows(out, p), out_sb[:, p.rest % 2, :, :]).then_inc(stored[p.rest % 2], 16)

            load(Place(None, 0))
            load(Place(None, 1))
            load_turned(Place(None, 0))
            with sp.Fori(1, G // 2) as pair:
                for u in range(2):
                    load(Place(pair, u))
                    load_turned(Place(pair, u - 1))
                    store(Place(pair, u - 2))
            load_turned(Place(None, G - 1))
            store(Place(None, G - 2))
            store(Place(None, G - 1))
            for par in range(2):
                sp.wait_ge(stored[par], 16 * (G // 2))

        @block.gpsimd
        def _(pool):
            g = nc.gpsimd
            g.memset(ones[:], 1.0).then_inc(const_ready, 1)
            g.memset(ident[:], 0.0).then_inc(const_ready, 1)
            g.memset(power[:, :], -0.5).then_inc(const_ready, 1)
            g.memset(count_w[:, 0, :], 1.0 / MASK).then_inc(const_ready, 1)
            g.memset(count_w[:, 1, :], -1.0 / MASK).then_inc(const_ready, 1)
            pool.wait_ge(const_ready, 5)
            g.affine_select(out=ident[:], in_=ident[:], compare_op=ALU.not_equal, fill=1.0, base=0,
                            pattern=[[-1, P]], channel_multiplier=1).then_inc(const_ready, 1)
            def deviation(p, stage, n):
                pool.wait_ge(stats_ready[stage], p.count(2, n + 1))
                g.tensor_tensor(rstd[stage][:], var_eps[stage][:], power[:], op=ALU.pow).then_inc(ln_ready[stage], 1)

            def add_bias(dst, src, rows, ready):
                g.tensor_tensor(dst, src, rows[:, :].unsqueeze(1).to_broadcast([P, C, D]),
                                op=ALU.add).then_inc(ready, 1)

            def step_a(p, step):
                if step == "stats0":
                    deviation(p, 0, 0)
                elif step == "stats1":
                    deviation(p, 0, 1)
                elif step == "dst1":
                    if p.pair is None and p.rest == 0:
                        pool.wait_ge(w_step, 13)
                    pool.wait_ge(x1_ready, p.count(1, 1))
                    add_bias(x1b[:], x1[:], b1_rows, x1b_ready)

            def step_b(p, step):
                if step == "stats2":
                    deviation(p, 1, 0)
                elif step == "features":
                    pool.wait_ge(x2_ready, p.count(1, 1))
                    add_bias(x2b[:], x2[:, p.rest % 2, :, :], b2_rows, x2b_ready)
                elif step == "stats3":
                    deviation(p, 1, 1)

            over_graphs(pool, "gpsimd", step_a, step_b)

        @block.scalar
        def _(act):
            s = nc.scalar

            def copy_turned(p, unit):
                act.wait_ge(turned, p.count(UNITS, unit + 1))
                head, c = divmod(unit, C)
                if head == 1 and c == 0:
                    act.wait_ge(av_done, p.count(2, 1))
                if head == 0 and c == 0 and p.before().exists():
                    act.wait_ge(av_done, p.before().count(2, 2))
                dst = pT[:, max(head - 1, 0), :, c * P:(c + 1) * P]
                s.activation(dst, turn[unit % 2][:, :].rearrange("p (j i) -> p j i", j=C),
                             ACT.Copy).then_inc(pT_copied, 1)

            def copy_hT(p, stage, n, dst, src):
                act.wait_ge(hT_ready[stage], p.count(2, n + 1))
                s.activation(dst[:, :], src[:, :], ACT.Copy).then_inc(hT_copied[stage], 1)

            def exponentials(p, unit):
                head, c = divmod(unit, C)
                act.wait_ge(logits_ready, p.count(UNITS, unit + 1))
                row = probs[:, (head % 2) * C + c, :]
                s.activation(row, row, ACT.Exp, bias=negm[:, head, c:c + 1],
                             accum_out=den[:, head, c:c + 1]).then_inc(probs_ready, 1)

            def small_branch(p, head, c):
                act.wait_ge(dst_read, p.count(HEADS, head + 1))
                if head or c > 1:
                    act.wait_ge(logits_ready, p.count(UNITS, head * C + c - 1))
                elif p.before().exists():
                    act.wait_ge(logits_ready, p.before().count(UNITS, UNITS))
                s.activation(lin[:, 1, :], probs[:, (head % 2) * C + c, :], ACT.Identity,
                             bias=s1_part[:, head, c:c + 1], scale=SLOPE).then_inc(small_ready, 1)

            def step_a(p, step):
                if step in ("rows0", "rows1"):
                    copy_hT(p, 0, int(step[4]), hT[0], turn0)
                elif step in ("values0", "values1"):
                    act.wait_ge(val_ready, p.count(2, int(step[6]) + 1))
                    s.activation(values[:, :, :].rearrange("p c d -> p (c d)"), av_bank[:, :],
                                 ACT.Copy).then_inc(val_copied, 1)
                elif step[0] == "u":
                    unit = int(step[1:])
                    if unit % 2 == 0:
                        small_branch(p, unit // C, unit % C + 1)
                    exponentials(p, unit)
                elif step[0] == "v" and int(step[1:]) not in (0, C):
                    copy_turned(p, int(step[1:]) - 1)
                elif step == "turned0":
                    copy_turned(p, C - 1)
                elif step == "turned1":
                    copy_turned(p, UNITS - 1)
                elif step == "sum1":
                    act.wait_ge(av_done, p.count(2, 2))
                    s.activation(avT[:, :], av_bank[:, :], ACT.Copy).then_inc(avT_copied, 1)

            def step_b(p, step):
                if step == "rows2":
                    copy_hT(p, 1, 0, hT[1], r_bank)
                elif step == "features":
                    s.activation(hTa[:, 0, :], r_bank[:, :], ACT.Identity,
                                 scale=sess_sb[:, 0:1]).then_inc(hTa_ready, 1)
                elif step[0] == "z":
                    j = int(step[1])
                    act.wait_ge(z_ready, p.count(C, j + 1))
                    s.activation(sess[:, j, :], z_banks[j][:, :], ACT.Copy).then_inc(z_copied, 1)
                elif step in S_STEPS:
                    j = int(step[1])
                    act.wait_ge(sess_ready, p.count(C, j + 1))
                    s.activation(sess[:, j, :], sess[:, j, :], ACT.Tanh, scale=0.5).then_inc(tanh_ready, 1)
                elif step == "rows3":
                    copy_hT(p, 1, 1, h3T, z_bank)
                    s.activation(half_state[:, :], z_bank[:, :], ACT.Copy, scale=0.5).then_inc(half_ready, 1)
                elif step[0] == "g":
                    gates(p, int(step[1]), int(step[2]))

            def gates(p, layer, part):
                n = layer + 1
                if part == 1:
                    act.wait_ge(agg_ready, p.count(LAYERS, n))
                    s.activation(aggT[:, :], n_bank[:, :], ACT.Copy).then_inc(agg_copied, 1)
                elif part == 2:
                    act.wait_ge(gh_ready, p.count(LAYERS, n))
                    s.activation(hid_n[:, :], h_bank[:, :], ACT.Identity, bias=half_bhn[:, 0:1],
                                 scale=0.5).then_inc(hid_copied, 1)
                elif part == 3:
                    act.wait_ge(gi_ready, p.count(3 * LAYERS, 3 * layer + 1))
                    s.activation(r_t[:, :], r_bank[:, :], ACT.Tanh, bias=gate_b[:, 0:1],
                                 scale=0.5).then_inc(gates_ready, 1)
                elif part == 4:
                    act.wait_ge(gi_ready, p.count(3 * LAYERS, 3 * layer + 3))
                    s.activation(z_t[:, :], z_bank[:, :], ACT.Tanh, bias=gate_b[:, 1:2],
                                 scale=0.5).then_inc(gates_ready, 1)
                elif part == 5:
                    act.wait_ge(pre_n_ready, p.count(LAYERS, n))
                    s.activation(n_t[:, :], g_tmp[:, :], ACT.Tanh, bias=gate_b[:, 2:3]).then_inc(n_ready, 1)
                elif part == 6 and layer < LAYERS - 1:
                    act.wait_ge(state_turned, p.count(LAYERS, n))
                    s.activation(hB[:, :, :].rearrange("p c d -> p (c d)"), h_bank[:, :],
                                 ACT.Copy).then_inc(state_copied, 1)
                elif part == 7 and layer < LAYERS - 1:
                    s.activation(half_state[:, :], hBT[:, layer % 2, :], ACT.Copy, scale=0.5).then_inc(half_ready, 1)

            act.wait_ge(w_step, 12)
            over_graphs(act, "scalar", step_a, step_b)

        @block.vector
        def _(dve):
            v = nc.vector
            wstep = [0]

            def w_own(ins):
                wstep[0] += 1
                ins.then_inc(w_step, 1)
                dve.wait_ge(w_step, wstep[0])

            dve.wait_ge(const_ready, 6)
            dve.wait_ge(w_loaded, 16 * (len(LOADS) + KINDS))
            w_own(v.memset(a1_heads[:, :, :], 0.0))
            for h in range(H1):
                q = slice(h * HD, (h + 1) * HD)
                last = v.tensor_copy(a1_heads[q, :, h], a1_sb[q, :])
            w_own(last)
            w_own(v.tensor_scalar(b1_rep[:], ones[:], b1_sb[:, 0:1], None, ALU.mult))
            v.tensor_scalar(diag[:, 0, :], ident[:], b1_sb[:, 0:1], None, ALU.mult)
            w_own(v.tensor_scalar(diag[:, 1, :], ident[:], b2_sb[:, 0:1], None, ALU.mult))
            v.tensor_tensor(gate_b[:, 0:2], bih_sb[:, 0:2], bhh_sb[:, 0:2], ALU.add)
            v.tensor_copy(gate_b[:, 2:3], bih_sb[:, 2:3])
            w_own(v.tensor_scalar(half_bhn[:], bhh_sb[:, 2:3], 0.5, None, ALU.mult))
            w_own(v.tensor_scalar(gate_b[:, 0:2], gate_b[:, 0:2], 0.5, None, ALU.mult))
            dve.wait_ge(pe_w, 1)
            v.tensor_copy(src_w[:, 0:1], dst_bank[:, 0:1])
            v.tensor_copy(dst_w[:, 0:1], dst_bank[:, 1:2])
            v.tensor_copy(src_w[:, 1:HEADS], dst_bank[:, 2:2 + H1])
            v.tensor_copy(dst_w[:, 1:HEADS], dst_bank[:, 2 + H1:2 + 2 * H1])
            w_own(v.tensor_copy(head_parts[:, :, :].rearrange("p a h -> p (a h)"), dst_bank[:, 16:16 + 2 * H1]))
            for h in range(HEADS):
                last = v.tensor_scalar(dst_rep[:, h, :], ones[:], dst_w[:, h:h + 1], None, ALU.mult)
            w_own(last)
            w_own(v.tensor_tensor(head_const[:], head_parts[:, 0, :], head_parts[:, 1, :], ALU.add))
            dve.wait_ge(pe_w, 2)
            v.tensor_copy(b1_rows[:], av_bank[:, 0:D])
            w_own(v.tensor_copy(b2_rows[:], av_bank[:, D:2 * D]))
            for i, bk in enumerate((r_bank, z_bank, n_bank)):
                dve.wait_ge(pe_w, 3 + i)
                last = v.tensor_copy(gi_w[:, i, :], bk[:, 0:3 * D])
            w_own(last)
            w_own(v.memset(settle_a[:], 0.0))
            w_own(v.memset(settle_a[:], 0.0))

            class Chain:

                def __init__(self, steps_done, per_graph):
                    self.steps_done, self.per_graph = steps_done, per_graph

                def start(self, p):
                    self.p, self.done = p, 0

                def wait(self):
                    dve.wait_ge(self.steps_done, self.p.count(self.per_graph, self.done))

                def link(self, ins):
                    self.done += 1
                    ins.then_inc(self.steps_done, 1)

                def own(self, ins):
                    self.link(ins)
                    self.wait()

                def settle(self, cell):
                    self.wait()
                    self.link(v.memset(cell[:, 0:1], 0.0))

            ca, cb, ck = Chain(dve_a, NA), Chain(dve_b, NB), Chain(dve_k, NK)

            def sums(stage, rows, chain, cell):
                for c in range(C):
                    last = v.bn_stats(stats[stage][:, c, :], rows[:, c, :])
                chain.own(last)
                chain.settle(cell)
                for c in range(C):
                    v.bn_aggr(moments[stage][:, c, :], stats[stage][:, c, :])
                chain.own(v.memset(cell[:, 2:3], 0.0))
                v.tensor_scalar(var_eps[stage][:, :], moments[stage][:, :, 1], EPS, None,
                                ALU.add).then_inc(stats_ready[stage], 1)

            def norm(p, n, stage, rows, dst, chain):
                dve.wait_ge(ln_ready[stage], p.count(2, n + 1))
                for c in range(C):
                    last = v.tensor_scalar(dst[:, c, :], rows[:, c, :], moments[stage][:, c, 0:1],
                                           rstd[stage][:, c:c + 1], ALU.subtract, ALU.mult)
                chain.own(last)
                v.tensor_scalar(dst[:, :, :], dst[:, :, :], 0.0, None, ALU.max).then_inc(hn_ready[stage], 1)

            def next_max(p, head, c):
                masks = mask0 if head == 0 else mask1
                if c == 0:
                    dve.wait_ge(dst_ready, p.count(HEADS, head + 1))
                if head >= 2:
                    dve.wait_ge(turned, p.count(UNITS, (head - 2) * C + c + 1))
                elif p.before().exists():
                    back = (HEADS - 1 if head == 0 else HEADS - 2) * C
                    dve.wait_ge(turned, p.before().count(UNITS, back + c + 1))
                ca.settle(settle_a)
                v.tensor_tensor_reduce(out=probs[:, (head % 2) * C + c, :], in0=dst_bank[:, :], in1=masks[:, c, :],
                                       scale=1.0, scalar=-3e38, op0=ALU.add, op1=ALU.max,
                                       accum_out=rmax[:, head, c:c + 1])

            def negative_max(head):
                ca.own(v.memset(settle_a[:, 1:2], 0.0))
                ca.own(v.tensor_tensor(mtmp[:, 0, :], rmax[:, head, :], s1[:, head, :], ALU.add))
                ca.own(v.tensor_scalar(mtmp[:, 1, :], mtmp[:, 0, :], -SLOPE, None, ALU.mult))
                v.scalar_tensor_tensor(negm[:, head, :], mtmp[:, 0, :], -1.0, mtmp[:, 1, :], ALU.mult,
                                       ALU.min).then_inc(dst_read, 1)

            def step_a(p, step):
                par = p.rest % 2
                if step == "stats0":
                    ca.start(p)
                    dve.wait_ge(x_loaded[par], p.count_of_parity(16, 16))
                    sums(0, xin[:, par, :, :], ca, settle_a)
                elif step == "rows0":
                    norm(p, 0, 0, xin[:, par, :, :], hn[0], ca)
                elif step == "mask0":
                    dve.wait_ge(adj_loaded, p.count(16, 16))
                    if p.before().exists():
                        dve.wait_ge(others_counted, p.before().count(1, 1))
                    v.tensor_scalar(mask0[:, :, :], adj_i[:, :, :], 0.0, -MASK, ALU.is_equal, ALU.mult)
                elif step == "mask1":
                    v.tensor_scalar(mask1[:, :, :], adj_i[:, :, :], 1.0, -MASK, ALU.not_equal, ALU.mult)
                elif step in ("values0", "values1"):
                    n = int(step[6])
                    heads = slice(0, 1) if n == 0 else slice(1, HEADS)
                    dve.wait_ge(val_ready, p.count(2, n + 1))
                    if n == 0:
                        last = v.tensor_copy(s1[:, 0, :], turn1[:, 0:C])
                    else:
                        last = v.tensor_tensor(s1[:, heads, :], turn1[:, 0:C * H1].rearrange("p (c h) -> p h c", h=H1),
                                               head_const[:, :].unsqueeze(2).to_broadcast([P, H1, C]), ALU.add)
                    last.then_inc(s1_copied, 1)
                    dve.wait_ge(s1_copied, p.count(2, n + 1))
                    ca.own(v.tensor_scalar(s1_part[:, heads, :], s1[:, heads, :], SLOPE, None, ALU.mult))
                elif step[0] in "mn" and len(step) == 2:
                    head, c = "mn".index(step[0]), int(step[1])
                    next_max(p, head, c)
                    if c == C - 1:
                        negative_max(head)
                elif step == "edges":
                    v.tensor_scalar(edges[:, par, :, :], adj_i[:, :, :], 0.0, 1.0, ALU.not_equal,
                                    ALU.mult).then_inc(adj_used, 1)
                elif step[0] == "u":
                    head, c = divmod(int(step[1:]), C)
                    row = probs[:, (head % 2) * C + c, :]
                    if c % 2:
                        dve.wait_ge(small_ready, p.count(UNITS // 2, (head * C + c + 1) // 2))
                    else:
                        if head or c:
                            dve.wait_ge(logits_ready, p.count(UNITS, head * C + c - 1))
                        ca.own(v.tensor_scalar(lin[:, 0, :], row, s1[:, head, c:c + 1], SLOPE, ALU.add, ALU.mult))
                    v.scalar_tensor_tensor(row, row, s1[:, head, c:c + 1], lin[:, c % 2, :], ALU.add,
                                           ALU.max).then_inc(logits_ready, 1)
                elif step[0] == "v":
                    head, c = divmod(int(step[1:]), C)
                    if 1 <= head < HEADS - 1:
                        for chunk in ((0,), (1, 2), (3,), ())[c]:
                            next_max(p, head + 1, chunk)
                        if c == 2:
                            negative_max(head + 1)
                elif step == "x1":
                    dve.wait_ge(probs_ready, p.count(UNITS, C))
                    v.tensor_scalar(alive[:, :], rmax[:, 0, :], -MASK / 2, None, ALU.is_gt)
                    ca.own(v.reciprocal(rden[:, 0, :], den[:, 0, :]))
                    ca.own(v.tensor_tensor(rden[:, 0, :], rden[:, 0, :], alive[:, :], ALU.mult))
                    dve.wait_ge(av_done, p.count(2, 1))
                    for c in range(C):
                        last = v.scalar_tensor_tensor(x1[:, c, :], av_bank[:, c * P:(c + 1) * P],
                                                      rden[:, 0, c:c + 1], xin[:, par, c, :], ALU.mult, ALU.add)
                    last.then_inc(x1_ready, 1)
                elif step == "stats1":
                    dve.wait_ge(x1_ready, p.count(1, 1))
                    sums(0, x1, ca, settle_a)
                elif step == "rows1":
                    norm(p, 1, 0, x1, hn[0], ca)
                elif step == "others":
                    dve.wait_ge(others_counted, p.count(1, 1))
                    v.tensor_reduce(other_kinds[:, par:par + 1], turn1[:, :], AX.X, ALU.max).then_inc(others_ready, 1)
                elif step == "x2":
                    dve.wait_ge(probs_ready, p.count(UNITS, UNITS))
                    ca.own(v.reciprocal(rden[:, 1:HEADS, :], den[:, 1:HEADS, :]))
                    dve.wait_ge(av_turned, p.count(1, 1))
                    ca.own(v.tensor_tensor(scaled[:, :, :].rearrange("p c (h e) -> p c h e", h=H1),
                                           turn0[:, :].rearrange("p (c h e) -> p c h e", c=C, h=H1),
                                           rden[:, 1:HEADS, :].rearrange("p h c -> p c h").unsqueeze(3)
                                           .to_broadcast([P, C, H1, HD]), ALU.mult))
                    dve.wait_ge(x1b_ready, p.count(1, 1))
                    v.tensor_tensor(x2[:, par, :, :], x1b[:, :, :], scaled[:, :, :], ALU.add).then_inc(x2_ready, 1)
                    assert ca.done == NA, ca.done

            def kinds_of(p, j, k):
                ck.own(v.tensor_scalar(kind_mask[:, :], adjt_i[:, j, :], float(k + 1), None, ALU.is_equal))
                n = REST * j + k - 1
                dve.wait_ge(zk_ready, p.count(REST * C, n + 1))
                ck.settle(settle_b)
                v.copy_predicated(sess[:, j, :], kind_mask[:, :], z_banks[n % 4][:, :]).then_inc(zk_used, 1)
                dve.wait_ge(zk_used, p.count(REST * C, n + 1))

            def step_b(p, step):
                par = p.rest % 2
                if step == "stats2":
                    cb.start(p)
                    ck.start(p)
                    dve.wait_ge(x2_ready, p.count(1, 1))
                    sums(1, x2[:, par, :, :], cb, settle_b)
                elif step == "rows2":
                    norm(p, 0, 1, x2[:, par, :, :], hn[1], cb)
                elif step == "mask2":
                    dve.wait_ge(adjt_loaded, p.count(16, 16))
                    v.tensor_scalar(any_kind[:, :, :], adjt_i[:, :, :], 1.0, 0.5, ALU.is_equal, ALU.mult)
                elif step == "kinds":
                    dve.wait_ge(others_ready, p.count(1, 1))
                    cb.link(v.memset(settle_b[:, 3:4], 0.0))
                    others = dve.value_load(other_kinds[0:1, par:par + 1])
                    with dve.If(others != 0):
                        dve.wait_ge(hT_copied[1], p.count(2, 1))
                        for k in range(1, KINDS):
                            last = v.tensor_scalar(hTa[:, k, :], hT[1][:, :], sess_sb[:, k:k + 1], None, ALU.mult)
                        last.then_inc(hTk_ready, 1)
                        dve.wait_ge(z_copied, p.count(C, C))
                        for j in range(C):
                            ck.own(v.tensor_scalar(upto[:, :], adjt_i[:, j, :], float(KINDS), 0.5, ALU.is_le, ALU.mult))
                            v.scalar_tensor_tensor(any_kind[:, j, :], adjt_i[:, j, :], 1.0, upto[:, :], ALU.is_ge,
                                                   ALU.mult)
                            for k in range(1, KINDS):
                                kinds_of(p, j, k)
                        ck.link(v.memset(settle_b[:, 1:2], 0.0))
                        assert ck.done == NK, ck.done
                    with dve.Else():
                        dve.sem_inc(hTk_ready, 1)
                        dve.sem_inc(zk_used, REST * C)
                        dve.sem_inc(dve_k, NK)
                    dve.wait_ge(dve_k, p.count(NK, NK))
                    cb.own(v.memset(settle_b[:, 1:2], 0.0))
                elif step in S_STEPS:
                    j = int(step[1])
                    dve.wait_ge(z_copied, p.count(C, j + 1))
                    v.scalar_tensor_tensor(sess[:, j, :], sess[:, j, :], SLOPE, sess[:, j, :], ALU.mult,
                                           ALU.max).then_inc(sess_ready, 1)
                elif step[0] == "w":
                    weights_of(p, int(step[1]))
                elif step == "x3":
                    v.memset(settle_b[:, 0:1], 0.0).then_inc(adjt_used, 1)
                    dve.wait_ge(x2b_ready, p.count(1, 1))
                    dve.wait_ge(av2_done, p.count(1, 1))
                    v.tensor_tensor(x3[:, :, :], r_bank[:, :].rearrange("p (c d) -> p c d", c=C), x2b[:, :, :],
                                    ALU.add).then_inc(x3_ready, 1)
                elif step == "stats3":
                    dve.wait_ge(x3_ready, p.count(1, 1))
                    sums(1, x3, cb, settle_b)
                elif step == "rows3":
                    norm(p, 1, 1, x3, h3, cb)
                elif step[0] == "g":
                    gates(p, int(step[1]), int(step[2]))
                    if step == "g27":
                        assert cb.done == NB, cb.done

            def weights_of(p, j):
                dve.wait_ge(tanh_ready, p.count(C, j + 1))
                v.scalar_tensor_tensor(alpha[:, j, :], sess[:, j, :], 1.0, any_kind[:, j, :], ALU.add,
                                       ALU.mult).then_inc(alpha_ready, 1)

            def gates(p, layer, part):
                par = p.rest % 2
                n = layer + 1
                new = hBT[:, layer % 2, :]
                if part == 3:
                    dve.wait_ge(hid_copied, p.count(LAYERS, n))
                    dve.wait_ge(gates_ready, p.count(2 * LAYERS, 2 * layer + 1))
                    cb.own(v.scalar_tensor_tensor(g_tmp[:, :], r_t[:, :], 1.0, hid_n[:, :], ALU.add, ALU.mult))
                    dve.wait_ge(gi_ready, p.count(3 * LAYERS, 3 * layer + 2))
                    v.tensor_tensor(g_tmp[:, :], g_tmp[:, :], n_bank[:, :], ALU.add).then_inc(pre_n_ready, 1)
                elif part == 4:
                    dve.wait_ge(half_ready, p.count(LAYERS, n))
                    dve.wait_ge(gates_ready, p.count(2 * LAYERS, 2 * layer + 2))
                    v.scalar_tensor_tensor(g_keep[:, :], z_t[:, :], 1.0, half_state[:, :], ALU.add, ALU.mult)
                elif part == 5:
                    dve.wait_ge(n_ready, p.count(LAYERS, n))
                    cb.own(v.scalar_tensor_tensor(g_tmp[:, :], z_t[:, :], -1.0, n_t[:, :], ALU.add, ALU.mult))
                    v.scalar_tensor_tensor(new, g_tmp[:, :], -0.5, g_keep[:, :], ALU.mult,
                                           ALU.add).then_inc(state_ready, 1)
                elif part == 6 and layer == LAYERS - 1:
                    dve.wait_ge(state_turned, p.count(LAYERS, n))
                    prev2 = p.before(2)
                    if prev2.exists():
                        dve.wait_ge(stored[par], prev2.count_of_parity(16, 16))
                    v.tensor_tensor(out_sb[:, par, :, :], h_bank[:, :].rearrange("p (c d) -> p c d", c=C),
                                    x3[:, :, :], ALU.add).then_inc(out_ready, 1)

            over_graphs(dve, "vector", step_a, step_b)

        @block.tensor
        def _(pe):
            t = nc.tensor
            pe.wait_ge(w_loaded, 16 * (len(LOADS) + KINDS))
            pe.wait_ge(const_ready, 6)
            pe.wait_ge(w_step, 4)
            t.matmul(dst_bank[:, 0:2], w0_sb[:], a0_sb[:], start=True, stop=True)
            heads_a = a1_heads[:, :, :].rearrange("p a h -> p (a h)")
            t.matmul(dst_bank[:, 2:2 + 2 * H1], w1_sb[:], heads_a, start=True, stop=True)
            t.matmul(dst_bank[:, 16:16 + 2 * H1], b1_rep[:], heads_a, start=True, stop=True).then_inc(pe_w, 1)
            t.matmul(av_bank[:, 0:D], ones[:], diag[:, 0, :], start=True, stop=True)
            t.matmul(av_bank[:, D:2 * D], ones[:], diag[:, 1, :], start=True, stop=True).then_inc(pe_w, 1)
            for i, bk in enumerate((r_bank, z_bank, n_bank)):
                t.matmul(bk[:, 0:3 * D], gate_wt_sb[:, i, :], w_iht_sb[:], start=True, stop=True).then_inc(pe_w, 1)

            def turn_rows(p, stage, n, dst, rows):
                pe.wait_ge(hn_ready[stage], p.count(2, n + 1))
                for c in range(C):
                    last = t.transpose(dst[:, c * P:(c + 1) * P], rows[:, c, :], ident[:])
                last.then_inc(hT_ready[stage], 1)

            def spread(p, head):
                if head >= 1:
                    pe.wait_ge(dst_read, p.count(HEADS, head))
                elif p.before().exists():
                    pe.wait_ge(dst_read, p.before().count(HEADS, HEADS))
                t.matmul(dst_bank[:, :], dst_rep[:, head, :], hT[0][:, :], start=True, stop=True).then_inc(dst_ready, 1)

            def project(p, n, wt, src, heads):
                for c in range(C):
                    t.matmul(turn1[:, c * heads:(c + 1) * heads], hT[0][:, c * P:(c + 1) * P], src, start=True,
                             stop=True)
                if n == 1:
                    pe.wait_ge(x1_ready, p.count(1, 1))
                elif p.before().exists():
                    pe.wait_ge(avT_copied, p.before().count(1, 1))
                for c in range(C):
                    last = t.matmul(av_bank[:, c * P:(c + 1) * P], hT[0][:, c * P:(c + 1) * P], wt, start=True,
                                    stop=True)
                last.then_inc(val_ready, 1)

            def turn_probs(p, unit):
                head, c = divmod(unit, C)
                pe.wait_ge(probs_ready, p.count(UNITS, unit + 1))
                if unit in (0, C):
                    pe.wait_ge(s1_copied, p.count(2, 1 + unit // C))
                if unit >= 2:
                    pe.wait_ge(pT_copied, p.count(UNITS, unit - 1))
                for j in range(C):
                    last = t.transpose(turn[unit % 2][:, j * P:(j + 1) * P],
                                       probs[:, (head % 2) * C + c, j * P:(j + 1) * P], ident[:])
                last.then_inc(turned, 1)

            def sum_l0(p, c):
                pe.wait_ge(pT_copied, p.count(UNITS, c + 1))
                if c == 0:
                    pe.wait_ge(val_copied, p.count(2, 1))
                for j in range(C):
                    last = t.matmul(av_bank[:, c * P:(c + 1) * P], pT[:, 0, j, c * P:(c + 1) * P],
                                    values[:, j, :], start=(j == 0), stop=(j == C - 1))
                return last

            def step_a(p, step):
                if step == "rows0":
                    if p.before().exists():
                        pe.wait_ge(x2_ready, p.before().count(1, 1))
                        pe.wait_ge(others_ready, p.before().count(1, 1))
                    turn_rows(p, 0, 0, turn0, hn[0])
                elif step in ("dst0", "dst1"):
                    pe.wait_ge(hT_copied[0], p.count(2, int(step[3]) + 1))
                    spread(p, int(step[3]))
                elif step == "values0":
                    project(p, 0, w0t_sb[:], src_w[:, 0:1], 1)
                elif step == "x1":
                    sum_l0(p, C - 1).then_inc(av_done, 1)
                elif step == "rows1":
                    pe.wait_ge(pT_copied, p.count(UNITS, C))
                    turn_rows(p, 0, 1, turn0, hn[0])
                elif step == "values1":
                    project(p, 1, w1t_sb[:], src_w[:, 1:HEADS], H1)
                elif step[0] == "u":
                    turn_probs(p, int(step[1:]))
                elif step[0] == "v":
                    head, c = divmod(int(step[1:]), C)
                    if head == 0 and c:
                        sum_l0(p, c - 1)
                    elif head and c == C - 2 and head + 2 < HEADS:
                        spread(p, head + 2)
                elif step == "n3":
                    spread(p, 2)
                elif step == "sum1":
                    pe.wait_ge(pT_copied, p.count(UNITS, UNITS))
                    pe.wait_ge(val_copied, p.count(2, 2))
                    for j in range(C):
                        for h in range(H1):
                            last = t.matmul(av_bank[h * HD:(h + 1) * HD, :], values[:, j, h * HD:(h + 1) * HD],
                                            pT[:, h, j, :], start=(j == 0), stop=(j == C - 1),
                                            skip_group_check=True)
                    last.then_inc(av_done, 1)
                elif step == "others":
                    for c in range(C):
                        for m, masks in enumerate((mask0, mask1)):
                            last = t.matmul(turn1[:, :], count_w[:, m, :], masks[:, c, :],
                                            start=(c == 0 and m == 0), stop=(c == C - 1 and m == 1))
                    last.then_inc(others_counted, 1)
                elif step == "x2":
                    pe.wait_ge(avT_copied, p.count(1, 1))
                    for c in range(C):
                        last = t.transpose(turn0[:, c * P:(c + 1) * P], avT[:, c * P:(c + 1) * P], ident[:])
                    last.then_inc(av_turned, 1)

            def step_b(p, step):
                prev = p.before()
                if step == "rows2":
                    if prev.exists():
                        pe.wait_ge(out_ready, prev.count(1, 1))
                    turn_rows(p, 1, 0, r_bank, hn[1])
                elif step[0] == "z":
                    j = int(step[1])
                    if j == 0:
                        pe.wait_ge(others_ready, p.count(1, 1))
                        pe.wait_ge(hTa_ready, p.count(1, 1))
                    t.matmul(z_banks[j][:, :], hT[1][:, j * P:(j + 1) * P], hTa[:, 0, :], start=True,
                             stop=True).then_inc(z_ready, 1)
                elif step == "kinds":
                    par = p.rest % 2
                    others = pe.value_load(other_kinds[0:1, par:par + 1])
                    with pe.If(others != 0):
                        pe.wait_ge(z_copied, p.count(C, C))
                        pe.wait_ge(hTk_ready, p.count(1, 1))
                        for j in range(C):
                            for k in range(1, KINDS):
                                n = REST * j + k - 1
                                if n >= 4:
                                    pe.wait_ge(zk_used, p.count(REST * C, n - 3))
                                t.matmul(z_banks[n % 4][:, :], hT[1][:, j * P:(j + 1) * P], hTa[:, k, :],
                                         start=True, stop=True).then_inc(zk_ready, 1)
                    with pe.Else():
                        pe.sem_inc(zk_ready, REST * C)
                elif step[0] == "w":
                    j = int(step[1])
                    pe.wait_ge(alpha_ready, p.count(C, j + 1))
                    for c in range(C):
                        last = t.matmul(r_bank[:, c * P:(c + 1) * P], alpha[:, j, c * P:(c + 1) * P],
                                        hn[1][:, j, :], start=(j == 0 and c == 0), stop=(j == C - 1),
                                        skip_group_check=True)
                    if j == C - 1:
                        last.then_inc(av2_done, 1)
                elif step == "rows3":
                    turn_rows(p, 1, 1, z_bank, h3)
                elif step[0] == "g":
                    gates(p, int(step[1]), int(step[2]))

            def gates(p, layer, part):
                par = p.rest % 2
                n = layer + 1
                stateT = h3T[:, :] if layer == 0 else hBT[:, (layer + 1) % 2, :]
                state = h3[:, :, :] if layer == 0 else hB[:, :, :]
                def hidden(bank, gate, stop=False):
                    return t.matmul(bank[:, :], w_hht_sb[:, gate * D:(gate + 1) * D], stateT, start=True, stop=stop)

                def joint(bank, gate, start=False):
                    t.matmul(bank[:, :], gi_w[:, layer, gate * D:(gate + 1) * D], aggT[:, :], start=start,
                             stop=True).then_inc(gi_ready, 1)

                if part == 0 and layer:
                    hidden(r_bank, 0)
                    hidden(z_bank, 1)
                elif part == 1:
                    if layer:
                        pe.wait_ge(state_copied, p.count(LAYERS - 1, layer))
                    for s in range(C):
                        last = t.matmul(n_bank[:, :], state[:, s, :], edges[:, par, s, :], start=(s == 0),
                                        stop=(s == C - 1))
                    last.then_inc(agg_ready, 1)
                    if layer == 0:
                        pe.wait_ge(hT_copied[1], p.count(2, 2))
                        pe.wait_ge(half_ready, p.count(LAYERS, 1))
                        hidden(r_bank, 0)
                        hidden(z_bank, 1)
                elif part == 2:
                    hidden(h_bank, 2, stop=True).then_inc(gh_ready, 1)
                elif part == 3:
                    pe.wait_ge(agg_copied, p.count(LAYERS, n))
                    joint(r_bank, 0)
                    joint(n_bank, 2, start=True)
                elif part == 4:
                    joint(z_bank, 1)
                elif part == 6:
                    pe.wait_ge(state_ready, p.count(LAYERS, n))
                    new = hBT[:, layer % 2, :]
                    for c in range(C):
                        last = t.transpose(h_bank[:, c * P:(c + 1) * P], new[:, c * P:(c + 1) * P], ident[:])
                    last.then_inc(state_turned, 1)

            pe.wait_ge(w_step, 12)
            over_graphs(pe, "tensor", step_a, step_b)


def kernel(x, adj, L0_gnn_W, L0_gnn_a, L1_gnn_W, L1_gnn_b, L1_gnn_a, L2_gnn_a0, L2_gnn_a1, L2_gnn_a2, L2_gnn_a3,
           L2_gnn_bias, L3_gnn_weight, L3_gnn_w_ih, L3_gnn_w_hh, L3_gnn_b_ih, L3_gnn_b_hh):
    import numpy as np
    import concourse.bacc as bacc
    from concourse.bass_utils import run_bass_kernel_spmd as run

    D = x.shape[-1]
    H1 = L1_gnn_a.shape[0]
    col = lambda a: np.asarray(a).reshape(D, 1)
    laid = {
        "x": x, "adj": adj, "adj_t": np.asarray(adj).swapaxes(1, 2),
        "w0": L0_gnn_W, "w0_t": np.asarray(L0_gnn_W).T, "a0": np.asarray(L0_gnn_a).reshape(2, D).T,
        "w1": L1_gnn_W, "w1_t": np.asarray(L1_gnn_W).T,
        "a1": np.asarray(L1_gnn_a).reshape(H1, 2, D // H1).transpose(0, 2, 1).reshape(D, 2),
        "b1": col(L1_gnn_b),
        "s0": col(L2_gnn_a0), "s1": col(L2_gnn_a1), "s2": col(L2_gnn_a2), "s3": col(L2_gnn_a3),
        "b2": col(L2_gnn_bias),
        "gate_w_t": np.asarray(L3_gnn_weight).transpose(2, 0, 1),
        "w_ih_t": np.asarray(L3_gnn_w_ih).T, "w_hh_t": np.asarray(L3_gnn_w_hh).T,
        "b_ih": np.asarray(L3_gnn_b_ih).reshape(3, D).T, "b_hh": np.asarray(L3_gnn_b_hh).reshape(3, D).T,
    }
    nc = bacc.Bacc("TRN2", target_bir_lowering=False, num_devices=1)
    arrays, aps = {}, {}
    for name, a in laid.items():
        a = np.ascontiguousarray(a)
        arrays[f"in_{name}"] = a
        aps[name] = nc.dram_tensor(f"in_{name}", a.shape, mybir.dt.from_np(a.dtype), kind="ExternalInput").ap()
    sess_a = [aps.pop(f"s{k}") for k in range(4)]
    out = nc.dram_tensor("out_0", x.shape, mybir.dt.float32, kind="ExternalOutput").ap()
    graph_layers(nc, **aps, sess_a=sess_a, out=out)
    return run(nc, [arrays], core_ids=[0]).results[0]["out_0"]
```

```python
from contextlib import ExitStack

import concourse.bass as bass
from concourse import mybir

fp32 = mybir.dt.float32
fp32r = mybir.dt.float32r
bf16 = mybir.dt.bfloat16
i32 = mybir.dt.int32
ALU = mybir.AluOpType
ACT = mybir.ActivationFunctionType
AX = mybir.AxisListType

P = 128
EPS = 1e-5
SLOPE = 0.2
MASK = 2.0 ** 56

A_STEPS = (
    ["stats0", "norm0", "rows0"]
    + ["mask0", "mask1"]
    + ["dst0", "src0"] + [f"m{c}" for c in range(4)]
    + ["values0", "max0"]
    + [f"{s}{n}" for n in range(4) for s in "uv"]
    + ["edges", "turned0", "x1"]
    + [f"others{n}" for n in range(4)]
    + ["stats1", "norm1", "rows1"]
    + ["dst1", "src1"] + [f"n{c}" for c in range(4)]
    + ["values1", "max1"]
    + [f"{s}{n}" for n in range(4, 20) for s in "uv"] + ["turned1"])
AGG_STEPS = tuple(f"agg{n}" for n in range(4))
LAST_STEPS = ("hidden_n", "joint_r", "joint_n", "hidden_z", "joint_z", "mix", "turn", "half")
GATE_STEPS = (AGG_STEPS + ("hidden_r",) + LAST_STEPS, ("hidden_r",) + AGG_STEPS + LAST_STEPS)
B_STEPS = (
    [f"sum{n}" for n in range(4)] + ["x2"]
    + ["stats2", "norm2", "rows2", "features", "mask2"]
    + [f"z{n}" for n in range(4)] + ["kinds"]
    + [f"s{n}" for n in range(4)]
    + [f"w{n}" for n in range(4)] + ["x3"]
    + ["stats3", "norm3", "rows3"]
    + [f"g{layer}_{part}" for layer in range(3) for part in GATE_STEPS[layer > 0]])
PLACES = {
    "tensor": (1, 1, 4, 8, 12, 19, 26, 27, 27, 28, 28, 28, 28, 28, 28, 28, 28, 28, 28, 29, 29, 29, 30, 34, 36, 38,
               38, 38, 38, 39, 39, 39, 39, 39, 40, 40, 40, 42, 45, 45, 47, 47, 47, 47, 48, 49, 49, 49, 49, 49, 49,
               53, 53, 54, 54, 55, 55, 55, 55, 58, 58, 58, 60, 63, 66, 66,),
    "vector": (1, 1, 5, 19, 19, 20, 20, 21, 21, 21, 24, 25, 25, 26, 27, 29, 29, 29, 29, 29, 29, 29, 29, 30, 32,
               34, 36, 41, 43, 43, 43, 43, 43, 45, 47, 48, 48, 48, 49, 50, 50, 52, 52, 52, 53, 53, 53, 53, 53, 54,
               54, 57, 58, 58, 58, 58, 58, 58, 62, 65, 65, 65, 65, 68, 71, 71,),
    "scalar": (1, 7, 11, 13, 13, 20, 23, 25, 26, 26, 26, 26, 26, 26, 26, 28, 28, 29, 29, 29, 29, 29, 36, 37, 37,
               37, 41, 42, 42, 42, 42, 42, 42, 42, 43, 44, 44, 45, 47, 50, 50, 50, 50, 50, 50, 50, 51, 51, 51, 52,
               52, 55, 55, 56, 56, 56, 57, 57, 58, 60, 62, 63, 63, 64, 72, 72,),
}
PLACES["gpsimd"] = PLACES["vector"]


def merged(engine):
    order = []
    for n in range(len(A_STEPS) + 1):
        order += [("B", step) for step, place in zip(B_STEPS, PLACES[engine]) if place == n]
        order += [("A", step) for step in A_STEPS[n:n + 1]]
    return order


class Place:

    def __init__(self, pair, rest):
        self.pair, self.rest = pair, rest

    def count(self, per_graph, within):
        fixed = self.rest * per_graph + within
        return fixed if self.pair is None else self.pair * (2 * per_graph) + fixed

    def count_of_parity(self, per_graph, within):
        fixed = (self.rest // 2) * per_graph + within
        return fixed if self.pair is None else self.pair * per_graph + fixed

    def index(self):
        return self.rest if self.pair is None else self.pair * 2 + self.rest

    def before(self, n=1):
        return Place(self.pair, self.rest - n)

    def exists(self):
        return self.pair is not None or self.rest >= 0


def graph_layers(nc, x, adj, adj_t, weights, out):
    G, N, D = x.shape
    C = N // P
    H1 = 4
    HD = D // H1
    HEADS = 1 + H1
    UNITS = HEADS * C
    KINDS = 4
    LAYERS = 3
    REST = KINDS - 1

    ctx = ExitStack()
    with ctx:
        def sb(name, shape, dt=fp32):
            return ctx.enter_context(nc.sbuf_tensor(name, shape, dt))

        def sem(name):
            return ctx.enter_context(nc.semaphore(name))

        ident = sb("ident", [P, P])
        ones = sb("ones", [P, P])
        diag = sb("diag", [P, 2, P])
        weights_sb = sb("weights_sb", [P, weights.shape[1]])
        column = [0]

        def part(width):
            column[0] += width
            return weights_sb[:, column[0] - width:column[0]]

        w0_sb, w0t_sb, a0_sb, w1_sb, w1t_sb, a1_sb = part(D), part(D), part(2), part(D), part(D), part(2)
        b1_sb, b2_sb, sess_sb = part(1), part(1), part(KINDS)
        gate_wt_sb = [part(D) for _ in range(LAYERS)]
        w_iht_sb, w_hht_sb, bih_sb, bhh_sb = part(3 * D), part(3 * D), part(3), part(3)
        a1_heads = sb("a1_heads", [P, 2, H1])
        b1_rep = sb("b1_rep", [P, P])
        src_w = sb("src_w", [P, HEADS])
        dst_w = sb("dst_w", [P, HEADS])
        dst_rep = sb("dst_rep", [P, HEADS, P])
        head_const = sb("head_const", [P, H1])
        head_parts = sb("head_parts", [P, 2, H1])
        b1_rows, b2_rows = sb("b1_rows", [P, D]), sb("b2_rows", [P, D])
        gi_w = sb("gi_w", [P, LAYERS, 3 * D])
        gate_b = sb("gate_b", [P, 3])
        half_bhn = sb("half_bhn", [P, 1])

        xin = sb("xin", [P, 2, C, D])
        adj_i = sb("adj_i", [P, C, N], i32)
        adjt_i = sb("adjt_i", [P, C, N], i32)
        mask0, mask1 = sb("mask0", [P, C, N], bf16), sb("mask1", [P, C, N], bf16)
        x1, x1b = sb("x1", [P, C, D]), sb("x1b", [P, C, D])
        stats = [sb(f"stats{n}", [P, C, 6]) for n in range(2)]
        moments = [sb(f"moments{n}", [P, C, 2]) for n in range(2)]
        var_eps, rstd = ([sb(f"{m}{n}", [P, C]) for n in range(2)] for m in ("var_eps", "rstd"))
        shift = sb("shift", [P, C])
        power, minus_one = sb("power", [P, C]), sb("minus_one", [P, C])
        hn = [sb(f"hn{n}", [P, C, D]) for n in range(2)]
        hT = [sb(f"hT{n}", [P, N]) for n in range(2)]
        values = [sb(f"values{n}", [P, C, D]) for n in range(2)]
        s1, s1_part = sb("s1", [P, HEADS, C]), sb("s1_part", [P, HEADS, C])
        rmax, negm, den = sb("rmax", [P, HEADS, C]), sb("negm", [P, HEADS, C]), sb("den", [P, HEADS, C])
        minus = sb("minus", [P, C])
        rden = sb("rden", [P, HEADS, C])
        alive = sb("alive", [P, C])
        probs = sb("probs", [P, 2 * C, N])
        lin = sb("lin", [P, 2, N])
        pT = sb("pT", [P, H1, C, N])
        avT = sb("avT", [P, N])
        scaled = sb("scaled", [P, C, D])
        settle_a, settle_b = sb("settle_a", [P, 4]), sb("settle_b", [P, 4])
        count_w = sb("count_w", [P, 2, P], bf16)

        x2 = sb("x2", [P, 2, C, D])
        edges = sb("edges", [P, 2, C, N], fp32r)
        other_kinds = sb("other_kinds", [P, 2], i32)

        x2b, x3 = sb("x2b", [P, C, D]), sb("x3", [P, C, D])
        hTa = sb("hTa", [P, N])
        sess = sb("sess", [P, C, N])
        alpha = sb("alpha", [P, C, N])
        kind_mask = sb("kind_mask", [P, N], i32)
        upto = sb("upto", [P, N])
        any_kind = sb("any_kind", [P, C, N])
        h3 = sb("h3", [P, C, D])
        h3T = sb("h3T", [P, N])
        aggT = sb("aggT", [P, N])
        hid_n = sb("hid_n", [P, N])
        r_t, z_t, n_t = sb("r_t", [P, N]), sb("z_t", [P, N]), sb("n_t", [P, N])
        g_tmp, g_keep = sb("g_tmp", [P, N]), sb("g_keep", [P, N])
        half_state = sb("half_state", [P, N])
        hBT = sb("hBT", [P, 2, N])
        state_hi, state_lo = sb("state_hi", [P, C, D], fp32r), sb("state_lo", [P, C, D], fp32r)
        out_sb = sb("out_sb", [P, 2, C, D])

        def bank(name):
            return ctx.enter_context(nc.psum_tensor(name, [P, N], fp32))

        dst_bank, turn0, turn1, av_bank = bank("dst_bank"), bank("turn0"), bank("turn1"), bank("av_bank")
        r_bank, z_bank, n_bank, h_bank = bank("r_bank"), bank("z_bank"), bank("n_bank"), bank("h_bank")
        turn = (turn0, turn1)
        z_banks = (r_bank, z_bank, n_bank, h_bank)

        w_loaded = sem("w_loaded")
        const_ready = sem("const_ready")
        w_step = sem("w_step")
        pe_w = sem("pe_w")
        gi_w_ready = sem("gi_w_ready")
        x_loaded = [sem("x_loaded0"), sem("x_loaded1")]
        adj_loaded, adjt_loaded = sem("adj_loaded"), sem("adjt_loaded")
        adj_used, adjt_used = sem("adj_used"), sem("adjt_used")
        stats_ready = [sem(f"stats_ready{n}") for n in range(2)]
        ln_ready = [sem(f"ln_ready{n}") for n in range(2)]
        pool_step = sem("pool_step")
        hn_ready = [sem(f"hn_ready{n}") for n in range(2)]
        hT_ready = [sem(f"hT_ready{n}") for n in range(2)]
        hT_copied = [sem(f"hT_copied{n}") for n in range(2)]
        val_ready, val_copied = sem("val_ready"), sem("val_copied")
        s1_copied = sem("s1_copied")
        dst_ready, dst_read = sem("dst_ready"), sem("dst_read")
        small_ready = sem("small_ready")
        logits_ready = sem("logits_ready")
        probs_ready = sem("probs_ready")
        turned = sem("turned")
        pT_copied = sem("pT_copied")
        l0_done, l1_done = sem("l0_done"), sem("l1_done")
        avT_copied, av_turned = sem("avT_copied"), sem("av_turned")
        x1_ready, x2_ready = sem("x1_ready"), sem("x2_ready")
        x1b_ready = sem("x1b_ready")
        others_counted, others_ready = sem("others_counted"), sem("others_ready")
        dve_a = sem("dve_a")
        x2b_ready = sem("x2b_ready")
        hTa_ready, hTk_ready = sem("hTa_ready"), sem("hTk_ready")
        z_ready, z_copied = sem("z_ready"), sem("z_copied")
        zk_ready, zk_used = sem("zk_ready"), sem("zk_used")
        dve_k = sem("dve_k")
        sess_ready, tanh_ready = sem("sess_ready"), sem("tanh_ready")
        alpha_ready = sem("alpha_ready")
        av2_done, x3_ready = sem("av2_done"), sem("x3_ready")
        gh_ready = sem("gh_ready")
        agg_ready, agg_copied = sem("agg_ready"), sem("agg_copied")
        hid_copied = sem("hid_copied")
        half_ready = sem("half_ready")
        gi_ready = sem("gi_ready")
        gates_ready = sem("gates_ready")
        pre_n_ready, n_ready = sem("pre_n_ready"), sem("n_ready")
        state_ready = sem("state_ready")
        state_turned = sem("state_turned")
        rest_ready = sem("rest_ready")
        state_copied = sem("state_copied")
        dve_b = sem("dve_b")
        out_ready = sem("out_ready")
        stored = [sem("stored0"), sem("stored1")]

        S_STEPS = tuple(f"s{n}" for n in range(C))
        NA = 67
        NB = 16
        NK = 29

        block = ctx.enter_context(nc.Block())

        def over_graphs(eng, engine, step_a, step_b):
            for step in A_STEPS:
                step_a(Place(None, 0), step)

            def both(pa, pb):
                for stage, step in merged(engine):
                    if stage == "A":
                        step_a(pa, step)
                    else:
                        step_b(pb, step)

            both(Place(None, 1), Place(None, 0))
            with eng.Fori(1, G // 2) as pair:
                for u in range(2):
                    both(Place(pair, u), Place(pair, u - 1))
            for step in B_STEPS:
                step_b(Place(None, G - 1), step)

        @block.sync
        def _(sp):
            sp.dma_start(weights_sb[:], weights).then_inc(w_loaded, 16)

            def rows(array, p):
                return array[bass.ds(p.index(), 1), :, :].rearrange("o (c p) n -> p (o c) n", p=P)

            def load(p):
                par = p.rest % 2
                prev, prev2 = p.before(), p.before(2)
                if prev.exists():
                    sp.wait_ge(adj_used, prev.count(1, 1))
                sp.dma_start(adj_i[:], rows(adj, p)).then_inc(adj_loaded, 16)
                if prev2.exists():
                    sp.wait_ge(x1_ready, prev2.count(1, 1))
                sp.dma_start(xin[:, par, :, :], rows(x, p)).then_inc(x_loaded[par], 16)

            def load_turned(p):
                if p.before().exists():
                    sp.wait_ge(adjt_used, p.before().count(1, 1))
                sp.dma_start(adjt_i[:], rows(adj_t, p)).then_inc(adjt_loaded, 16)

            def store(p):
                sp.wait_ge(out_ready, p.count(1, 1))
                sp.dma_start(rows(out, p), out_sb[:, p.rest % 2, :, :]).then_inc(stored[p.rest % 2], 16)

            load(Place(None, 0))
            load(Place(None, 1))
            load_turned(Place(None, 0))
            with sp.Fori(1, G // 2) as pair:
                for u in range(2):
                    load(Place(pair, u))
                    load_turned(Place(pair, u - 1))
                    store(Place(pair, u - 2))
            load_turned(Place(None, G - 1))
            store(Place(None, G - 2))
            store(Place(None, G - 1))
            for par in range(2):
                sp.wait_ge(stored[par], 16 * (G // 2))

        @block.gpsimd
        def _(pool):
            g = nc.gpsimd
            g.memset(ones[:], 1.0).then_inc(const_ready, 1)
            g.memset(ident[:], 0.0).then_inc(const_ready, 1)
            g.memset(power[:, :], -0.5).then_inc(const_ready, 1)
            g.memset(minus_one[:, :], -1.0).then_inc(const_ready, 1)
            g.memset(count_w[:, 0, :], 1.0 / MASK).then_inc(const_ready, 1)
            g.memset(count_w[:, 1, :], -1.0 / MASK).then_inc(const_ready, 1)
            pool.wait_ge(const_ready, 6)
            g.affine_select(out=ident[:], in_=ident[:], compare_op=ALU.not_equal, fill=1.0, base=0,
                            pattern=[[-1, P]], channel_multiplier=1).then_inc(const_ready, 1)
            def deviation(p, stage, n):
                pool.wait_ge(stats_ready[stage], p.count(2, n + 1))
                if stage == 0:
                    g.tensor_tensor(rstd[0][:], var_eps[0][:], power[:], op=ALU.pow).then_inc(ln_ready[0], 1)
                    return
                g.tensor_tensor(shift[:], moments[1][:, :, 0], minus_one[:], op=ALU.mult)
                g.tensor_tensor(rstd[1][:], var_eps[1][:], power[:], op=ALU.pow).then_inc(pool_step, 1)
                pool.wait_ge(pool_step, p.count(2, n + 1))
                g.tensor_tensor(shift[:], shift[:], rstd[1][:], op=ALU.mult).then_inc(ln_ready[1], 1)

            def add_bias(dst, src, rows, ready):
                g.tensor_tensor(dst, src, rows[:, :].unsqueeze(1).to_broadcast([P, C, D]),
                                op=ALU.add).then_inc(ready, 1)

            def step_a(p, step):
                if step == "stats0":
                    deviation(p, 0, 0)
                elif step == "stats1":
                    deviation(p, 0, 1)
                elif step == "dst1":
                    if p.pair is None and p.rest == 0:
                        pool.wait_ge(w_step, 11)
                    pool.wait_ge(x1_ready, p.count(1, 1))
                    if p.before().exists():
                        pool.wait_ge(x2_ready, p.before().count(1, 1))
                    add_bias(x1b[:], x1[:], b1_rows, x1b_ready)

            def step_b(p, step):
                if step == "stats2":
                    deviation(p, 1, 0)
                elif step == "features":
                    pool.wait_ge(x2_ready, p.count(1, 1))
                    add_bias(x2b[:], x2[:, p.rest % 2, :, :], b2_rows, x2b_ready)
                elif step == "stats3":
                    deviation(p, 1, 1)

            over_graphs(pool, "gpsimd", step_a, step_b)

        @block.scalar
        def _(act):
            s = nc.scalar

            def copy_turned(p, unit):
                act.wait_ge(turned, p.count(UNITS, unit + 1))
                head, c = divmod(unit, C)
                if head == 1 and c == 0:
                    act.wait_ge(l0_done, p.count(1, 1))
                if head == 0 and c == 0 and p.before().exists():
                    act.wait_ge(l1_done, p.before().count(1, 1))
                dst = pT[:, max(head - 1, 0), :, c * P:(c + 1) * P]
                s.activation(dst, turn[unit % 2][:, :].rearrange("p (j i) -> p j i", j=C),
                             ACT.Copy).then_inc(pT_copied, 1)

            def norm(p, n, rows, dst):
                act.wait_ge(ln_ready[1], p.count(2, n + 1))
                for c in range(C):
                    last = s.activation(dst[:, c, :], rows[:, c, :], ACT.Relu, bias=shift[:, c:c + 1],
                                        scale=rstd[1][:, c:c + 1])
                last.then_inc(hn_ready[1], 1)

            def copy_hT(p, stage, n, dst, src, function=ACT.Copy):
                act.wait_ge(hT_ready[stage], p.count(2, n + 1))
                s.activation(dst[:, :], src[:, :], function).then_inc(hT_copied[stage], 1)

            def exponentials(p, unit):
                head, c = divmod(unit, C)
                act.wait_ge(logits_ready, p.count(UNITS, unit + 1))
                if unit == C and p.before().exists():
                    act.wait_ge(x2_ready, p.before().count(1, 1))
                row = probs[:, (head % 2) * C + c, :]
                s.activation(row, row, ACT.Exp, bias=negm[:, head, c:c + 1],
                             accum_out=den[:, head, c:c + 1]).then_inc(probs_ready, 1)

            def small_branch(p, head, c):
                act.wait_ge(dst_read, p.count(HEADS, head + 1))
                if head or c > 1:
                    act.wait_ge(logits_ready, p.count(UNITS, head * C + c - 1))
                elif p.before().exists():
                    act.wait_ge(logits_ready, p.before().count(UNITS, UNITS))
                s.activation(lin[:, 1, :], probs[:, (head % 2) * C + c, :], ACT.Identity,
                             bias=s1_part[:, head, c:c + 1], scale=SLOPE).then_inc(small_ready, 1)

            def step_a(p, step):
                if step in ("rows0", "rows1"):
                    copy_hT(p, 0, int(step[4]), hT[0], turn0, ACT.Relu)
                elif step in ("values0", "values1"):
                    act.wait_ge(val_ready, p.count(2, int(step[6]) + 1))
                    s.activation(values[int(step[6])][:, :, :].rearrange("p c d -> p (c d)"), av_bank[:, :],
                                 ACT.Copy).then_inc(val_copied, 1)
                elif step[0] == "u":
                    unit = int(step[1:])
                    if unit % 2 == 0:
                        small_branch(p, unit // C, unit % C + 1)
                    exponentials(p, unit)
                elif step[0] == "v" and int(step[1:]) not in (0, C):
                    copy_turned(p, int(step[1:]) - 1)
                elif step == "turned0":
                    copy_turned(p, C - 1)
                elif step == "turned1":
                    copy_turned(p, UNITS - 1)

            def step_b(p, step):
                if step == "sum3":
                    act.wait_ge(l1_done, p.count(1, 1))
                    s.activation(avT[:, :], n_bank[:, :], ACT.Copy).then_inc(avT_copied, 1)
                elif step == "norm2":
                    norm(p, 0, x2[:, p.rest % 2, :, :], hn[1])
                elif step == "norm3":
                    norm(p, 1, x3, h3)
                elif step == "rows2":
                    copy_hT(p, 1, 0, hT[1], r_bank)
                elif step == "features":
                    s.activation(hTa[:, :], r_bank[:, :], ACT.Identity,
                                 scale=sess_sb[:, 0:1]).then_inc(hTa_ready, 1)
                elif step[0] == "z":
                    j = int(step[1])
                    act.wait_ge(z_ready, p.count(C, j + 1))
                    s.activation(sess[:, j, :], z_banks[j][:, :], ACT.Copy).then_inc(z_copied, 1)
                elif step in S_STEPS:
                    j = int(step[1])
                    act.wait_ge(sess_ready, p.count(C, j + 1))
                    s.activation(sess[:, j, :], sess[:, j, :], ACT.Tanh, scale=0.5).then_inc(tanh_ready, 1)
                elif step == "rows3":
                    copy_hT(p, 1, 1, h3T, z_bank)
                    s.activation(half_state[:, :], z_bank[:, :], ACT.Copy, scale=0.5).then_inc(half_ready, 1)
                elif step[0] == "g":
                    gates(p, int(step[1]), step[3:])

            def gates(p, layer, part):
                n = layer + 1
                if part == "agg3":
                    act.wait_ge(agg_ready, p.count(LAYERS, n))
                    s.activation(aggT[:, :], n_bank[:, :], ACT.Copy).then_inc(agg_copied, 1)
                elif part == "hidden_n":
                    act.wait_ge(gh_ready, p.count(LAYERS, n))
                    s.activation(hid_n[:, :], h_bank[:, :], ACT.Identity, bias=half_bhn[:, 0:1],
                                 scale=0.5).then_inc(hid_copied, 1)
                elif part == "joint_r":
                    act.wait_ge(gi_ready, p.count(3 * LAYERS, 3 * layer + 1))
                    s.activation(r_t[:, :], r_bank[:, :], ACT.Tanh, bias=gate_b[:, 0:1],
                                 scale=0.5).then_inc(gates_ready, 1)
                elif part == "joint_z":
                    act.wait_ge(gi_ready, p.count(3 * LAYERS, 3 * layer + 3))
                    s.activation(z_t[:, :], z_bank[:, :], ACT.Tanh, bias=gate_b[:, 1:2],
                                 scale=0.5).then_inc(gates_ready, 1)
                elif part == "mix":
                    act.wait_ge(pre_n_ready, p.count(LAYERS, n))
                    s.activation(n_t[:, :], g_tmp[:, :], ACT.Tanh, bias=gate_b[:, 2:3]).then_inc(n_ready, 1)
                elif part == "turn" and layer < LAYERS - 1:
                    act.wait_ge(state_turned, p.count(LAYERS, n))
                    s.activation(state_hi[:, :, :].rearrange("p c d -> p (c d)"), h_bank[:, :],
                                 ACT.Copy).then_inc(state_copied, 1)
                elif part == "half" and layer < LAYERS - 1:
                    s.activation(half_state[:, :], hBT[:, layer % 2, :], ACT.Copy, scale=0.5).then_inc(half_ready, 1)

            for i, bk in enumerate((r_bank, z_bank, n_bank)):
                act.wait_ge(pe_w, 3 + i)
                s.activation(gi_w[:, i, :], bk[:, 0:3 * D], ACT.Copy).then_inc(gi_w_ready, 1)
            act.wait_ge(w_step, 11)
            over_graphs(act, "scalar", step_a, step_b)

        @block.vector
        def _(dve):
            v = nc.vector
            wstep = [0]

            def w_own(ins):
                wstep[0] += 1
                ins.then_inc(w_step, 1)
                dve.wait_ge(w_step, wstep[0])

            dve.wait_ge(const_ready, 7)
            dve.wait_ge(w_loaded, 16)
            w_own(v.memset(a1_heads[:, :, :], 0.0))
            for h in range(H1):
                q = slice(h * HD, (h + 1) * HD)
                last = v.tensor_copy(a1_heads[q, :, h], a1_sb[q, :])
            w_own(last)
            w_own(v.tensor_scalar(b1_rep[:], ones[:], b1_sb[:, 0:1], None, ALU.mult))
            v.tensor_scalar(diag[:, 0, :], ident[:], b1_sb[:, 0:1], None, ALU.mult)
            w_own(v.tensor_scalar(diag[:, 1, :], ident[:], b2_sb[:, 0:1], None, ALU.mult))
            v.tensor_tensor(gate_b[:, 0:2], bih_sb[:, 0:2], bhh_sb[:, 0:2], ALU.add)
            v.tensor_copy(gate_b[:, 2:3], bih_sb[:, 2:3])
            w_own(v.tensor_scalar(half_bhn[:], bhh_sb[:, 2:3], 0.5, None, ALU.mult))
            w_own(v.tensor_scalar(gate_b[:, 0:2], gate_b[:, 0:2], 0.5, None, ALU.mult))
            dve.wait_ge(pe_w, 1)
            v.tensor_copy(src_w[:, 0:1], dst_bank[:, 0:1])
            v.tensor_copy(dst_w[:, 0:1], dst_bank[:, 1:2])
            v.tensor_copy(src_w[:, 1:HEADS], dst_bank[:, 2:2 + H1])
            v.tensor_copy(dst_w[:, 1:HEADS], dst_bank[:, 2 + H1:2 + 2 * H1])
            w_own(v.tensor_copy(head_parts[:, :, :].rearrange("p a h -> p (a h)"), dst_bank[:, 16:16 + 2 * H1]))
            for h in range(HEADS):
                last = v.tensor_scalar(dst_rep[:, h, :], ones[:], dst_w[:, h:h + 1], None, ALU.mult)
            w_own(last)
            w_own(v.tensor_tensor(head_const[:], head_parts[:, 0, :], head_parts[:, 1, :], ALU.add))
            dve.wait_ge(pe_w, 2)
            v.tensor_copy(b1_rows[:], av_bank[:, 0:D])
            w_own(v.tensor_copy(b2_rows[:], av_bank[:, D:2 * D]))
            w_own(v.memset(settle_a[:], 0.0))

            class Chain:

                def __init__(self, steps_done, per_graph):
                    self.steps_done, self.per_graph = steps_done, per_graph

                def start(self, p):
                    self.p, self.done = p, 0

                def wait(self):
                    dve.wait_ge(self.steps_done, self.p.count(self.per_graph, self.done))

                def link(self, ins):
                    self.done += 1
                    ins.then_inc(self.steps_done, 1)

                def own(self, ins):
                    self.link(ins)
                    self.wait()

                def settle(self, cell):
                    self.wait()
                    self.link(v.memset(cell[:, 0:1], 0.0))

            ca, cb, ck = Chain(dve_a, NA), Chain(dve_b, NB), Chain(dve_k, NK)

            def sums(stage, rows, chain, cell):
                for c in range(C):
                    last = v.bn_stats(stats[stage][:, c, :], rows[:, c, :])
                chain.own(last)
                chain.settle(cell)
                for c in range(C):
                    v.bn_aggr(moments[stage][:, c, :], stats[stage][:, c, :])
                chain.own(v.memset(cell[:, 2:3], 0.0))
                v.tensor_scalar(var_eps[stage][:, :], moments[stage][:, :, 1], EPS, None,
                                ALU.add).then_inc(stats_ready[stage], 1)

            def norm(p, n, rows):
                dve.wait_ge(ln_ready[0], p.count(2, n + 1))
                for c in range(C):
                    last = v.tensor_scalar(hn[0][:, c, :], rows[:, c, :], moments[0][:, c, 0:1],
                                           rstd[0][:, c:c + 1], ALU.subtract, ALU.mult)
                last.then_inc(hn_ready[0], 1)

            def next_max(p, head, c):
                masks = mask0 if head == 0 else mask1
                if c == 0:
                    dve.wait_ge(dst_ready, p.count(HEADS, head + 1))
                if head >= 2:
                    dve.wait_ge(turned, p.count(UNITS, (head - 2) * C + c + 1))
                elif p.before().exists():
                    back = (HEADS - 1 if head == 0 else HEADS - 2) * C
                    dve.wait_ge(turned, p.before().count(UNITS, back + c + 1))
                ca.settle(settle_a)
                ca.link(v.tensor_tensor_reduce(out=probs[:, (head % 2) * C + c, :], in0=dst_bank[:, :],
                                               in1=masks[:, c, :], scale=1.0, scalar=-3e38, op0=ALU.add,
                                               op1=ALU.max, accum_out=rmax[:, head, c:c + 1]))

            def negative_max(head):
                ca.wait()
                ca.own(v.scalar_tensor_tensor(minus[:, :], rmax[:, head, :], -1.0, s1[:, head, :], ALU.mult,
                                              ALU.subtract))
                v.scalar_tensor_tensor(negm[:, head, :], minus[:, :], SLOPE, minus[:, :], ALU.mult,
                                       ALU.min).then_inc(dst_read, 1)

            def step_a(p, step):
                par = p.rest % 2
                if step == "stats0":
                    ca.start(p)
                    dve.wait_ge(x_loaded[par], p.count_of_parity(16, 16))
                    sums(0, xin[:, par, :, :], ca, settle_a)
                elif step == "norm0":
                    norm(p, 0, xin[:, par, :, :])
                elif step == "norm1":
                    norm(p, 1, x1)
                elif step == "mask0":
                    dve.wait_ge(adj_loaded, p.count(16, 16))
                    if p.before().exists():
                        dve.wait_ge(others_counted, p.before().count(1, 1))
                    ca.link(v.tensor_scalar(mask0[:, :, :], adj_i[:, :, :], 0.0, -MASK, ALU.is_equal, ALU.mult))
                elif step == "mask1":
                    ca.link(v.tensor_scalar(mask1[:, :, :], adj_i[:, :, :], 1.0, -MASK, ALU.not_equal, ALU.mult))
                elif step in ("values0", "values1"):
                    n = int(step[6])
                    heads = slice(0, 1) if n == 0 else slice(1, HEADS)
                    dve.wait_ge(val_ready, p.count(2, n + 1))
                    if n == 0:
                        last = v.tensor_copy(s1[:, 0, :], turn1[:, 0:C])
                    else:
                        last = v.tensor_tensor(s1[:, heads, :], turn1[:, 0:C * H1].rearrange("p (c h) -> p h c", h=H1),
                                               head_const[:, :].unsqueeze(2).to_broadcast([P, H1, C]), ALU.add)
                    last.then_inc(s1_copied, 1)
                    dve.wait_ge(s1_copied, p.count(2, n + 1))
                    ca.own(v.tensor_scalar(s1_part[:, heads, :], s1[:, heads, :], SLOPE, None, ALU.mult))
                elif step[0] in "mn" and len(step) == 2:
                    head, c = "mn".index(step[0]), int(step[1])
                    next_max(p, head, c)
                elif step in ("max0", "max1"):
                    negative_max(int(step[3]))
                elif step == "edges":
                    v.tensor_scalar(edges[:, par, :, :], adj_i[:, :, :], 0.0, 1.0, ALU.not_equal,
                                    ALU.mult).then_inc(adj_used, 1)
                elif step[0] == "u":
                    head, c = divmod(int(step[1:]), C)
                    row = probs[:, (head % 2) * C + c, :]
                    if c % 2:
                        dve.wait_ge(small_ready, p.count(UNITS // 2, (head * C + c + 1) // 2))
                    else:
                        if head or c:
                            dve.wait_ge(logits_ready, p.count(UNITS, head * C + c - 1))
                        ca.own(v.tensor_scalar(lin[:, 0, :], row, s1[:, head, c:c + 1], SLOPE, ALU.add, ALU.mult))
                    v.scalar_tensor_tensor(row, row, s1[:, head, c:c + 1], lin[:, c % 2, :], ALU.add,
                                           ALU.max).then_inc(logits_ready, 1)
                elif step[0] == "v":
                    head, c = divmod(int(step[1:]), C)
                    if 1 <= head < HEADS - 1:
                        for chunk in ((0,), (1, 2), (3,), ())[c]:
                            next_max(p, head + 1, chunk)
                        if c == 2:
                            negative_max(head + 1)
                elif step == "x1":
                    dve.wait_ge(probs_ready, p.count(UNITS, C))
                    v.tensor_scalar(alive[:, :], rmax[:, 0, :], -MASK / 2, None, ALU.is_gt)
                    ca.own(v.reciprocal(rden[:, 0, :], den[:, 0, :]))
                    ca.own(v.tensor_tensor(rden[:, 0, :], rden[:, 0, :], alive[:, :], ALU.mult))
                    dve.wait_ge(l0_done, p.count(1, 1))
                    for c in range(C):
                        last = v.scalar_tensor_tensor(x1[:, c, :], av_bank[:, c * P:(c + 1) * P],
                                                      rden[:, 0, c:c + 1], xin[:, par, c, :], ALU.mult, ALU.add)
                    last.then_inc(x1_ready, 1)
                elif step == "stats1":
                    dve.wait_ge(x1_ready, p.count(1, 1))
                    sums(0, x1, ca, settle_a)
                elif step == "others3":
                    dve.wait_ge(others_counted, p.count(1, 1))
                    v.tensor_reduce(other_kinds[:, par:par + 1], turn1[:, :], AX.X, ALU.max).then_inc(others_ready, 1)
                if step == A_STEPS[-1]:
                    assert ca.done == NA, ca.done

            def kinds_of(p, j, k):
                ck.own(v.tensor_scalar(kind_mask[:, :], adjt_i[:, j, :], float(k + 1), None, ALU.is_equal))
                n = REST * j + k - 1
                dve.wait_ge(zk_ready, p.count(REST * C, n + 1))
                ck.settle(settle_b)
                v.copy_predicated(sess[:, j, :], kind_mask[:, :], z_banks[n % 4][:, :]).then_inc(zk_used, 1)
                dve.wait_ge(zk_used, p.count(REST * C, n + 1))

            def step_b(p, step):
                par = p.rest % 2
                if step == "x2":
                    cb.start(p)
                    ck.start(p)
                    dve.wait_ge(probs_ready, p.count(UNITS, UNITS))
                    cb.own(v.reciprocal(rden[:, 1:HEADS, :], den[:, 1:HEADS, :]))
                    dve.wait_ge(av_turned, p.count(1, 1))
                    cb.own(v.tensor_tensor(scaled[:, :, :].rearrange("p c (h e) -> p c h e", h=H1),
                                           r_bank[:, :].rearrange("p (c h e) -> p c h e", c=C, h=H1),
                                           rden[:, 1:HEADS, :].rearrange("p h c -> p c h").unsqueeze(3)
                                           .to_broadcast([P, C, H1, HD]), ALU.mult))
                    dve.wait_ge(x1b_ready, p.count(1, 1))
                    v.tensor_tensor(x2[:, par, :, :], x1b[:, :, :], scaled[:, :, :], ALU.add).then_inc(x2_ready, 1)
                elif step == "stats2":
                    dve.wait_ge(x2_ready, p.count(1, 1))
                    sums(1, x2[:, par, :, :], cb, settle_b)
                elif step == "mask2":
                    dve.wait_ge(adjt_loaded, p.count(16, 16))
                    v.tensor_scalar(any_kind[:, :, :], adjt_i[:, :, :], 1.0, 0.5, ALU.is_equal, ALU.mult)
                elif step == "kinds":
                    dve.wait_ge(others_ready, p.count(1, 1))
                    cb.link(v.memset(settle_b[:, 3:4], 0.0))
                    others = dve.value_load(other_kinds[0:1, par:par + 1])
                    with dve.If(others != 0):
                        dve.wait_ge(hT_copied[1], p.count(2, 1))
                        for k in range(1, KINDS):
                            last = v.tensor_scalar(alpha[:, k, :], hT[1][:, :], sess_sb[:, k:k + 1], None, ALU.mult)
                        last.then_inc(hTk_ready, 1)
                        dve.wait_ge(z_copied, p.count(C, C))
                        for j in range(C):
                            ck.own(v.tensor_scalar(upto[:, :], adjt_i[:, j, :], float(KINDS), 0.5, ALU.is_le, ALU.mult))
                            v.scalar_tensor_tensor(any_kind[:, j, :], adjt_i[:, j, :], 1.0, upto[:, :], ALU.is_ge,
                                                   ALU.mult)
                            for k in range(1, KINDS):
                                kinds_of(p, j, k)
                        ck.link(v.memset(settle_b[:, 1:2], 0.0))
                        assert ck.done == NK, ck.done
                    with dve.Else():
                        dve.sem_inc(hTk_ready, 1)
                        dve.sem_inc(zk_used, REST * C)
                        dve.sem_inc(dve_k, NK)
                    dve.wait_ge(dve_k, p.count(NK, NK))
                    cb.own(v.memset(settle_b[:, 1:2], 0.0))
                elif step in S_STEPS:
                    j = int(step[1])
                    dve.wait_ge(z_copied, p.count(C, j + 1))
                    v.scalar_tensor_tensor(sess[:, j, :], sess[:, j, :], SLOPE, sess[:, j, :], ALU.mult,
                                           ALU.max).then_inc(sess_ready, 1)
                elif step[0] == "w":
                    weights_of(p, int(step[1]))
                elif step == "x3":
                    v.memset(settle_b[:, 0:1], 0.0).then_inc(adjt_used, 1)
                    dve.wait_ge(x2b_ready, p.count(1, 1))
                    dve.wait_ge(av2_done, p.count(1, 1))
                    v.tensor_tensor(x3[:, :, :], r_bank[:, :].rearrange("p (c d) -> p c d", c=C), x2b[:, :, :],
                                    ALU.add).then_inc(x3_ready, 1)
                elif step == "stats3":
                    dve.wait_ge(x3_ready, p.count(1, 1))
                    sums(1, x3, cb, settle_b)
                elif step[0] == "g":
                    gates(p, int(step[1]), step[3:])
                    if step == "g2_half":
                        assert cb.done == NB, cb.done

            def weights_of(p, j):
                dve.wait_ge(tanh_ready, p.count(C, j + 1))
                v.scalar_tensor_tensor(alpha[:, j, :], sess[:, j, :], 1.0, any_kind[:, j, :], ALU.add,
                                       ALU.mult).then_inc(alpha_ready, 1)

            def gates(p, layer, part):
                par = p.rest % 2
                n = layer + 1
                new = hBT[:, layer % 2, :]
                if part == "joint_r":
                    dve.wait_ge(hid_copied, p.count(LAYERS, n))
                    dve.wait_ge(gates_ready, p.count(2 * LAYERS, 2 * layer + 1))
                    cb.own(v.scalar_tensor_tensor(g_tmp[:, :], r_t[:, :], 1.0, hid_n[:, :], ALU.add, ALU.mult))
                elif part == "joint_n":
                    dve.wait_ge(gi_ready, p.count(3 * LAYERS, 3 * layer + 2))
                    v.tensor_tensor(g_tmp[:, :], g_tmp[:, :], n_bank[:, :], ALU.add).then_inc(pre_n_ready, 1)
                elif part == "joint_z":
                    dve.wait_ge(half_ready, p.count(LAYERS, n))
                    dve.wait_ge(gates_ready, p.count(2 * LAYERS, 2 * layer + 2))
                    v.scalar_tensor_tensor(g_keep[:, :], z_t[:, :], 1.0, half_state[:, :], ALU.add, ALU.mult)
                elif part == "mix":
                    dve.wait_ge(n_ready, p.count(LAYERS, n))
                    cb.own(v.scalar_tensor_tensor(g_tmp[:, :], z_t[:, :], -1.0, n_t[:, :], ALU.add, ALU.mult))
                    v.scalar_tensor_tensor(new, g_tmp[:, :], -0.5, g_keep[:, :], ALU.mult,
                                           ALU.add).then_inc(state_ready, 1)
                elif part == "turn" and layer < LAYERS - 1:
                    dve.wait_ge(state_copied, p.count(LAYERS - 1, n))
                    v.tensor_tensor(state_lo[:, :, :].rearrange("p c d -> p (c d)"), h_bank[:, :],
                                    state_hi[:, :, :].rearrange("p c d -> p (c d)").bitcast(fp32),
                                    ALU.subtract).then_inc(rest_ready, 1)
                elif part == "turn":
                    dve.wait_ge(state_turned, p.count(LAYERS, n))
                    prev2 = p.before(2)
                    if prev2.exists():
                        dve.wait_ge(stored[par], prev2.count_of_parity(16, 16))
                    v.tensor_tensor(out_sb[:, par, :, :], h_bank[:, :].rearrange("p (c d) -> p c d", c=C),
                                    x3[:, :, :], ALU.add).then_inc(out_ready, 1)

            over_graphs(dve, "vector", step_a, step_b)

        @block.tensor
        def _(pe):
            t = nc.tensor
            pe.wait_ge(w_loaded, 16)
            pe.wait_ge(const_ready, 7)
            pe.wait_ge(w_step, 4)
            t.matmul(dst_bank[:, 0:2], w0_sb[:], a0_sb[:], start=True, stop=True)
            heads_a = a1_heads[:, :, :].rearrange("p a h -> p (a h)")
            t.matmul(dst_bank[:, 2:2 + 2 * H1], w1_sb[:], heads_a, start=True, stop=True)
            t.matmul(dst_bank[:, 16:16 + 2 * H1], b1_rep[:], heads_a, start=True, stop=True).then_inc(pe_w, 1)
            t.matmul(av_bank[:, 0:D], ones[:], diag[:, 0, :], start=True, stop=True)
            t.matmul(av_bank[:, D:2 * D], ones[:], diag[:, 1, :], start=True, stop=True).then_inc(pe_w, 1)
            for i, bk in enumerate((r_bank, z_bank, n_bank)):
                t.matmul(bk[:, 0:3 * D], gate_wt_sb[i], w_iht_sb[:], start=True, stop=True).then_inc(pe_w, 1)

            def turn_rows(p, stage, n, dst, rows):
                pe.wait_ge(hn_ready[stage], p.count(2, n + 1))
                for c in range(C):
                    last = t.transpose(dst[:, c * P:(c + 1) * P], rows[:, c, :], ident[:])
                last.then_inc(hT_ready[stage], 1)

            def spread(p, head):
                if head >= 1:
                    pe.wait_ge(dst_read, p.count(HEADS, head))
                elif p.before().exists():
                    pe.wait_ge(dst_read, p.before().count(HEADS, HEADS))
                t.matmul(dst_bank[:, :], dst_rep[:, head, :], hT[0][:, :], start=True, stop=True).then_inc(dst_ready, 1)

            def sources(p, n, src, heads):
                for c in range(C):
                    t.matmul(turn1[:, c * heads:(c + 1) * heads], hT[0][:, c * P:(c + 1) * P], src, start=True,
                             stop=True)

            def project(p, n, wt):
                if n == 1:
                    pe.wait_ge(x1_ready, p.count(1, 1))
                elif p.before().exists():
                    pe.wait_ge(val_copied, p.before().count(2, 2))
                for c in range(C):
                    last = t.matmul(av_bank[:, c * P:(c + 1) * P], hT[0][:, c * P:(c + 1) * P], wt, start=True,
                                    stop=True)
                last.then_inc(val_ready, 1)

            def turn_probs(p, unit):
                head, c = divmod(unit, C)
                pe.wait_ge(probs_ready, p.count(UNITS, unit + 1))
                if unit in (0, C):
                    pe.wait_ge(s1_copied, p.count(2, 1 + unit // C))
                if unit >= 2:
                    pe.wait_ge(pT_copied, p.count(UNITS, unit - 1))
                for j in range(C):
                    last = t.transpose(turn[unit % 2][:, j * P:(j + 1) * P],
                                       probs[:, (head % 2) * C + c, j * P:(j + 1) * P], ident[:])
                last.then_inc(turned, 1)

            def sum_l0(p, c):
                pe.wait_ge(pT_copied, p.count(UNITS, c + 1))
                if c == 0:
                    pe.wait_ge(val_copied, p.count(2, 1))
                for j in range(C):
                    last = t.matmul(av_bank[:, c * P:(c + 1) * P], pT[:, 0, j, c * P:(c + 1) * P],
                                    values[0][:, j, :], start=(j == 0), stop=(j == C - 1))
                return last

            def step_a(p, step):
                if step == "rows0":
                    if p.before().exists():
                        pe.wait_ge(pT_copied, p.before().count(UNITS, UNITS))
                    turn_rows(p, 0, 0, turn0, hn[0])
                elif step in ("dst0", "dst1"):
                    pe.wait_ge(hT_copied[0], p.count(2, int(step[3]) + 1))
                    spread(p, int(step[3]))
                elif step == "values0":
                    project(p, 0, w0t_sb[:])
                elif step == "src0":
                    sources(p, 0, src_w[:, 0:1], 1)
                elif step == "src1":
                    pe.wait_ge(others_ready, p.count(1, 1))
                    sources(p, 1, src_w[:, 1:HEADS], H1)
                elif step == "x1":
                    sum_l0(p, C - 1).then_inc(l0_done, 1)
                elif step == "rows1":
                    pe.wait_ge(pT_copied, p.count(UNITS, C))
                    turn_rows(p, 0, 1, turn0, hn[0])
                elif step == "values1":
                    project(p, 1, w1t_sb[:])
                elif step[0] == "u":
                    turn_probs(p, int(step[1:]))
                elif step[0] == "v":
                    head, c = divmod(int(step[1:]), C)
                    if head == 0 and c:
                        sum_l0(p, c - 1)
                    elif head and c == C - 2 and head + 2 < HEADS:
                        spread(p, head + 2)
                elif step == "max1":
                    spread(p, 2)
                elif step[:6] == "others":
                    c = int(step[6])
                    if c == 0:
                        pe.wait_ge(pT_copied, p.count(UNITS, C))
                    for m, masks in enumerate((mask0, mask1)):
                        last = t.matmul(turn1[:, :], count_w[:, m, :], masks[:, c, :], start=(c == 0 and m == 0),
                                        stop=(c == C - 1 and m == 1))
                    if c == C - 1:
                        last.then_inc(others_counted, 1)

            def step_b(p, step):
                prev = p.before()
                if step[:3] == "sum":
                    j = int(step[3])
                    if j == 0:
                        if prev.exists():
                            pe.wait_ge(out_ready, prev.count(1, 1))
                        pe.wait_ge(pT_copied, p.count(UNITS, UNITS))
                        pe.wait_ge(val_copied, p.count(2, 2))
                    for h in range(H1):
                        last = t.matmul(n_bank[h * HD:(h + 1) * HD, :], values[1][:, j, h * HD:(h + 1) * HD],
                                        pT[:, h, j, :], start=(j == 0), stop=(j == C - 1), skip_group_check=True)
                    if j == C - 1:
                        last.then_inc(l1_done, 1)
                elif step == "x2":
                    pe.wait_ge(avT_copied, p.count(1, 1))
                    for c in range(C):
                        last = t.transpose(r_bank[:, c * P:(c + 1) * P], avT[:, c * P:(c + 1) * P], ident[:])
                    last.then_inc(av_turned, 1)
                elif step == "rows2":
                    turn_rows(p, 1, 0, r_bank, hn[1])
                elif step[0] == "z":
                    j = int(step[1])
                    if j == 0:
                        pe.wait_ge(others_ready, p.count(1, 1))
                        pe.wait_ge(hTa_ready, p.count(1, 1))
                    t.matmul(z_banks[j][:, :], hT[1][:, j * P:(j + 1) * P], hTa[:, :], start=True,
                             stop=True).then_inc(z_ready, 1)
                elif step == "kinds":
                    par = p.rest % 2
                    others = pe.value_load(other_kinds[0:1, par:par + 1])
                    with pe.If(others != 0):
                        pe.wait_ge(z_copied, p.count(C, C))
                        pe.wait_ge(hTk_ready, p.count(1, 1))
                        for j in range(C):
                            for k in range(1, KINDS):
                                n = REST * j + k - 1
                                if n >= 4:
                                    pe.wait_ge(zk_used, p.count(REST * C, n - 3))
                                t.matmul(z_banks[n % 4][:, :], hT[1][:, j * P:(j + 1) * P], alpha[:, k, :],
                                         start=True, stop=True).then_inc(zk_ready, 1)
                    with pe.Else():
                        pe.sem_inc(zk_ready, REST * C)
                elif step[0] == "w":
                    j = int(step[1])
                    pe.wait_ge(alpha_ready, p.count(C, j + 1))
                    for c in range(C):
                        last = t.matmul(r_bank[:, c * P:(c + 1) * P], alpha[:, j, c * P:(c + 1) * P],
                                        hn[1][:, j, :], start=(j == 0 and c == 0), stop=(j == C - 1),
                                        skip_group_check=True)
                    if j == C - 1:
                        last.then_inc(av2_done, 1)
                elif step == "rows3":
                    turn_rows(p, 1, 1, z_bank, h3)
                elif step[0] == "g":
                    gates(p, int(step[1]), step[3:])

            def gates(p, layer, part):
                par = p.rest % 2
                n = layer + 1
                stateT = h3T[:, :] if layer == 0 else hBT[:, (layer + 1) % 2, :]
                def hidden(bank, gate, stop=False):
                    return t.matmul(bank[:, :], w_hht_sb[:, gate * D:(gate + 1) * D], stateT, start=True, stop=stop)

                def joint(bank, gate, start=False):
                    t.matmul(bank[:, :], gi_w[:, layer, gate * D:(gate + 1) * D], aggT[:, :], start=start,
                             stop=True).then_inc(gi_ready, 1)

                if part == "hidden_r":
                    if layer == 0:
                        pe.wait_ge(hT_copied[1], p.count(2, 2))
                        pe.wait_ge(half_ready, p.count(LAYERS, 1))
                    hidden(r_bank, 0)
                elif part == "hidden_z":
                    hidden(z_bank, 1)
                elif part[:3] == "agg":
                    s = int(part[3])
                    if layer == 0:
                        last = t.matmul(n_bank[:, :], h3[:, s, :], edges[:, par, s, :].bitcast(fp32), start=(s == 0),
                                        stop=(s == C - 1))
                    else:
                        if s == 0:
                            pe.wait_ge(state_copied, p.count(LAYERS - 1, layer))
                        elif s == 2:
                            pe.wait_ge(rest_ready, p.count(LAYERS - 1, layer))
                        for n in (2 * s, 2 * s + 1):
                            rows = (state_hi if n < C else state_lo)[:, n % C, :]
                            last = t.matmul(n_bank[:, :], rows, edges[:, par, n % C, :], start=(n == 0),
                                            stop=(n == 2 * C - 1))
                    if s == C - 1:
                        last.then_inc(agg_ready, 1)
                elif part == "hidden_n":
                    if layer:
                        pe.wait_ge(rest_ready, p.count(LAYERS - 1, layer))
                    hidden(h_bank, 2, stop=True).then_inc(gh_ready, 1)
                elif part == "joint_r":
                    pe.wait_ge(agg_copied, p.count(LAYERS, n))
                    joint(r_bank, 0)
                elif part == "joint_n":
                    joint(n_bank, 2, start=True)
                elif part == "joint_z":
                    joint(z_bank, 1)
                elif part == "turn":
                    pe.wait_ge(state_ready, p.count(LAYERS, n))
                    new = hBT[:, layer % 2, :]
                    for c in range(C):
                        last = t.transpose(h_bank[:, c * P:(c + 1) * P], new[:, c * P:(c + 1) * P], ident[:])
                    last.then_inc(state_turned, 1)

            pe.wait_ge(w_step, 11)
            pe.wait_ge(gi_w_ready, LAYERS)
            over_graphs(pe, "tensor", step_a, step_b)


def kernel(x, adj, L0_gnn_W, L0_gnn_a, L1_gnn_W, L1_gnn_b, L1_gnn_a, L2_gnn_a0, L2_gnn_a1, L2_gnn_a2, L2_gnn_a3,
           L2_gnn_bias, L3_gnn_weight, L3_gnn_w_ih, L3_gnn_w_hh, L3_gnn_b_ih, L3_gnn_b_hh):
    import numpy as np
    import concourse.bacc as bacc
    from concourse.bass_utils import run_bass_kernel_spmd as run

    D = x.shape[-1]
    H1 = L1_gnn_a.shape[0]
    LAYERS = L3_gnn_weight.shape[0]
    columns = [L0_gnn_W, L0_gnn_W.T, L0_gnn_a.reshape(2, D).T, L1_gnn_W, L1_gnn_W.T,
               L1_gnn_a.reshape(H1, 2, D // H1).transpose(0, 2, 1).reshape(D, 2), L1_gnn_b, L2_gnn_bias,
               L2_gnn_a0, L2_gnn_a1, L2_gnn_a2, L2_gnn_a3, *(L3_gnn_weight[i].T for i in range(LAYERS)),
               L3_gnn_w_ih.T, L3_gnn_w_hh.T, L3_gnn_b_ih.reshape(3, D).T, L3_gnn_b_hh.reshape(3, D).T]
    laid = {"x": x, "adj": adj, "adj_t": adj.swapaxes(1, 2),
            "weights": np.concatenate([a.reshape(D, -1) for a in columns], axis=1)}
    nc = bacc.Bacc("TRN2", target_bir_lowering=False, num_devices=1)
    arrays, aps = {}, {}
    for name, a in laid.items():
        a = np.ascontiguousarray(a)
        arrays[f"in_{name}"] = a
        aps[name] = nc.dram_tensor(f"in_{name}", a.shape, mybir.dt.from_np(a.dtype), kind="ExternalInput").ap()
    out = nc.dram_tensor("out_0", x.shape, mybir.dt.float32, kind="ExternalOutput").ap()
    graph_layers(nc, **aps, out=out)
    return run(nc, [arrays], core_ids=[0]).results[0]["out_0"]
```
